# Optimizing a Trainium2 kernel written in Bass

```python
import numpy as np
import jax
import jax.numpy as jnp

def _softmax(x, axis=-1):
    return jax.nn.softmax(x, axis=axis)

def _gelu(x):
    return jax.nn.gelu(x, approximate=True)

def _silu(x):
    return jax.nn.silu(x)

def _sigmoid(x):
    return jax.nn.sigmoid(x)

def _layernorm(x, axis=-1, eps=1e-05):
    m = jnp.mean(x, axis=axis, keepdims=True)
    v = jnp.var(x, axis=axis, keepdims=True)
    return (x - m) / jnp.sqrt(v + eps)

def _scatter_add(tgt, idx, src, axis=0):
    return tgt.at[idx].add(src)

def _segment_sum(src, seg, n):
    return jax.ops.segment_sum(src, seg, n)
kernel_name = 'mk_recurrent_d1_jaxref_r8_0c49fc'

def setup_inputs(seed: int=0):
    np.random.seed(seed)
    _w = jnp.asarray

    def _L0_attn_setup():
        import jax, jax.numpy as jnp
        import numpy as np
        B, S, H = (1, 256, 512)
        NH = 32
        QK_NOPE, QK_ROPE, V_DIM = (128, 64, 128)
        Q_LORA, KV_LORA = (192, 64)
        EPS = 1e-06

        def _rms_norm(x, w):
            return x * jax.lax.rsqrt(jnp.mean(x * x, axis=-1, keepdims=True) + EPS) * w

        def _rope_cos_sin(seqlen, dim):
            freqs = 1.0 / 10000.0 ** (jnp.arange(0, dim, 2, dtype=jnp.float32) / dim)
            t = jnp.arange(seqlen, dtype=jnp.float32)
            ang = jnp.outer(t, freqs)
            return (jnp.cos(ang), jnp.sin(ang))

        def _apply_rope(x, cos, sin):
            x1 = x[..., 0::2]
            x2 = x[..., 1::2]
            r1 = x1 * cos - x2 * sin
            r2 = x1 * sin + x2 * cos
            return jnp.stack([r1, r2], axis=-1).reshape(x.shape)
        key = jax.random.key(seed)
        ks = jax.random.split(key, 7)
        s = 0.02
        return {'x': jax.random.normal(ks[0], (B, S, H), jnp.float32), 'wq_a': jax.random.normal(ks[1], (Q_LORA, H), jnp.float32) * s, 'q_norm_w': jnp.ones((Q_LORA,), jnp.float32), 'wq_b': jax.random.normal(ks[2], (NH * (QK_NOPE + QK_ROPE), Q_LORA), jnp.float32) * s, 'wkv_a': jax.random.normal(ks[3], (KV_LORA + QK_ROPE, H), jnp.float32) * s, 'kv_norm_w': jnp.ones((KV_LORA,), jnp.float32), 'wkv_b': jax.random.normal(ks[4], (NH * (QK_NOPE + V_DIM), KV_LORA), jnp.float32) * s, 'wo': jax.random.normal(ks[5], (H, NH * V_DIM), jnp.float32) * s}
    _L0_attn_in = _L0_attn_setup()

    def _L0_ffn_setup():
        import jax, jax.numpy as jnp
        import numpy as np
        B, S, D, O, E, R = (2, 512, 512, 512, 8, 16)
        TOP_K = 2
        SCALING = 32.0 / 16.0
        key = jax.random.key(seed)
        k = jax.random.split(key, 6)
        x = jax.random.normal(k[0], (B, S, D), dtype=jnp.float32)
        W_base = jax.random.normal(k[1], (O, D), dtype=jnp.float32) * 0.02
        b_base = jax.random.normal(k[2], (O,), dtype=jnp.float32) * 0.02
        W_router = jax.random.normal(k[3], (E, D), dtype=jnp.float32) * 0.01
        lora_A = jax.random.normal(k[4], (E, R, D), dtype=jnp.float32) * (1.0 / np.sqrt(D))
        lora_B = jax.random.normal(k[5], (E, O, R), dtype=jnp.float32) * 0.02
        return {'x': x, 'W_base': W_base, 'b_base': b_base, 'W_router': W_router, 'lora_A': lora_A, 'lora_B': lora_B}
    _L0_ffn_in = _L0_ffn_setup()
    _d = {'L0_attn_x': _L0_attn_in['x'], 'L0_attn_wq_a': _L0_attn_in['wq_a'], 'L0_attn_q_norm_w': _L0_attn_in['q_norm_w'], 'L0_attn_wq_b': _L0_attn_in['wq_b'], 'L0_attn_wkv_a': _L0_attn_in['wkv_a'], 'L0_attn_kv_norm_w': _L0_attn_in['kv_norm_w'], 'L0_attn_wkv_b': _L0_attn_in['wkv_b'], 'L0_attn_wo': _L0_attn_in['wo'], 'L0_ffn_W_base': _L0_ffn_in['W_base'], 'L0_ffn_b_base': _L0_ffn_in['b_base'], 'L0_ffn_W_router': _L0_ffn_in['W_router'], 'L0_ffn_lora_A': _L0_ffn_in['lora_A'], 'L0_ffn_lora_B': _L0_ffn_in['lora_B']}
    _x0 = _d['L0_attn_x']
    _d['L0_attn_x'] = jax.random.normal(jax.random.fold_in(jax.random.key(seed), 1), (2, 512, 512), dtype=_x0.dtype)
    del _x0
    return _d

def reference(L0_attn_x, L0_attn_wq_a, L0_attn_q_norm_w, L0_attn_wq_b, L0_attn_wkv_a, L0_attn_kv_norm_w, L0_attn_wkv_b, L0_attn_wo, L0_ffn_W_base, L0_ffn_b_base, L0_ffn_W_router, L0_ffn_lora_A, L0_ffn_lora_B):

    def _L0_attn_ref(x, wq_a, q_norm_w, wq_b, wkv_a, kv_norm_w, wkv_b, wo):
        import jax, jax.numpy as jnp
        import numpy as np
        B, S, H = (1, 256, 512)
        NH = 32
        QK_NOPE, QK_ROPE, V_DIM = (128, 64, 128)
        Q_LORA, KV_LORA = (192, 64)
        EPS = 1e-06

        def _rms_norm(x, w):
            return x * jax.lax.rsqrt(jnp.mean(x * x, axis=-1, keepdims=True) + EPS) * w

        def _rope_cos_sin(seqlen, dim):
            freqs = 1.0 / 10000.0 ** (jnp.arange(0, dim, 2, dtype=jnp.float32) / dim)
            t = jnp.arange(seqlen, dtype=jnp.float32)
            ang = jnp.outer(t, freqs)
            return (jnp.cos(ang), jnp.sin(ang))

        def _apply_rope(x, cos, sin):
            x1 = x[..., 0::2]
            x2 = x[..., 1::2]
            r1 = x1 * cos - x2 * sin
            r2 = x1 * sin + x2 * cos
            return jnp.stack([r1, r2], axis=-1).reshape(x.shape)
        b, s, _ = x.shape
        cos, sin = _rope_cos_sin(s, QK_ROPE)
        q = _rms_norm(x @ wq_a.T, q_norm_w) @ wq_b.T
        q = q.reshape(b, s, NH, QK_NOPE + QK_ROPE)
        q_nope, q_pe = (q[..., :QK_NOPE], q[..., QK_NOPE:])
        q_pe = _apply_rope(q_pe, cos[None, :, None, :], sin[None, :, None, :])
        kv = x @ wkv_a.T
        kv_c, k_pe = (kv[..., :KV_LORA], kv[..., KV_LORA:])
        k_pe = _apply_rope(k_pe, cos[None, :, :], sin[None, :, :])
        kv_up = _rms_norm(kv_c, kv_norm_w) @ wkv_b.T
        kv_up = kv_up.reshape(b, s, NH, QK_NOPE + V_DIM)
        k_nope, v = (kv_up[..., :QK_NOPE], kv_up[..., QK_NOPE:])
        scale = 1.0 / jnp.sqrt(jnp.float32(QK_NOPE + QK_ROPE))
        scores = (jnp.einsum('bshd,bthd->bhst', q_nope, k_nope) + jnp.einsum('bshd,btd->bhst', q_pe, k_pe)) * scale
        causal = jnp.tril(jnp.ones((s, s), bool))
        scores = jnp.where(causal[None, None], scores, jnp.finfo(scores.dtype).min)
        probs = jax.nn.softmax(scores, axis=-1)
        out = jnp.einsum('bhst,bthd->bshd', probs, v).reshape(b, s, NH * V_DIM)
        return out @ wo.T

    def _L0_ffn_ref(x, W_base, b_base, W_router, lora_A, lora_B):
        import jax, jax.numpy as jnp
        import numpy as np
        B, S, D, O, E, R = (2, 512, 512, 512, 8, 16)
        TOP_K = 2
        SCALING = 32.0 / 16.0
        d = x.shape[-1]
        n_experts = W_router.shape[0]
        xf = x.reshape(-1, d)
        logits = xf @ W_router.T
        probs = jax.nn.softmax(logits, axis=-1)
        topk_p, topk_i = jax.lax.top_k(probs, TOP_K)
        topk_p = topk_p / jnp.sum(topk_p, axis=-1, keepdims=True)
        w = jnp.sum(jax.nn.one_hot(topk_i, n_experts, dtype=xf.dtype) * topk_p[..., None], axis=1)
        h = jnp.einsum('td,erd->ter', xf, lora_A)
        lora_out = jnp.einsum('ter,eor,te->to', h, lora_B, w) * SCALING
        base = x @ W_base.T + b_base
        return base + lora_out.reshape(x.shape[:-1] + (W_base.shape[0],))
    x = L0_attn_x
    xn = _layernorm(x, axis=-1)
    s = _L0_attn_ref(xn, L0_attn_wq_a, L0_attn_q_norm_w, L0_attn_wq_b, L0_attn_wkv_a, L0_attn_kv_norm_w, L0_attn_wkv_b, L0_attn_wo)
    g = _silu(_L0_ffn_ref(xn, L0_ffn_W_base, L0_ffn_b_base, L0_ffn_W_router, L0_ffn_lora_A, L0_ffn_lora_B))
    x = x + s * g
    return x

_drawn_inputs = setup_inputs


def setup_inputs(seed=0):
    import zlib

    import numpy as np

    out = dict(_drawn_inputs(seed))
    spreads = {'L0_attn_q_norm_w': (1.0, 0.6), 'L0_attn_kv_norm_w': (1.0, 0.6)}
    factors = {'L0_attn_wq_a': 8.0,
     'L0_attn_wq_b': 8.0,
     'L0_attn_wkv_a': 5.975,
     'L0_attn_wkv_b': 4.929,
     'L0_attn_wo': 6.521,
     'L0_ffn_W_base': 8.0,
     'L0_ffn_b_base': 26.484,
     'L0_ffn_W_router': 8.0,
     'L0_ffn_lora_A': 8.0,
     'L0_ffn_lora_B': 8.0}
    for name, (base, spread) in spreads.items():
        noise = np.random.default_rng([zlib.crc32(name.encode()), seed]).standard_normal(out[name].shape)
        drawn = base * np.exp(spread * noise) if base else spread * noise
        out[name] = jnp.asarray(drawn.astype(out[name].dtype))
    for name, factor in factors.items():
        out[name] = (out[name] * factor).astype(out[name].dtype)
    return out
```

```python
import concourse.bass as bass
from concourse import mybir
from contextlib import ExitStack

f32 = mybir.dt.float32
f32r = mybir.dt.float32r
f16 = mybir.dt.float16
bf16 = mybir.dt.bfloat16
u32 = mybir.dt.uint32
ALU = mybir.AluOpType
ACT = mybir.ActivationFunctionType
AX = mybir.AxisListType

P = 128
B, S, D = 2, 512, 512
NT = B * S // P
KD = D // P
NH, NOPE, ROPE, VD = 32, 128, 64, 128
QL, KL = 192, 64
NE, R = 8, 16
EPS_LN, EPS_RMS = 1e-5, 1e-6
LORA_SCALE = 32.0 / 16.0
NQ = S // P
HP = 2
NP = NH // HP
GP = 2
NI = NP // GP
UPI = GP * B * HP
NU = NI * UPI
SPI = UPI * NQ
NN = NU * NQ
OPI = GP * B
NO = NI * OPI
C1 = QL + KL + ROPE + NE * R + NE
cQ, cC, cK, cH, cL = 0, QL, QL + KL, QL + KL + ROPE, QL + KL + ROPE + NE * R
PS = 1024.0
MASKED = -1e37
SWAP = [i ^ 1 for i in range(32)]

wQ = 0
wR = wQ + HP * 256
wK = wR + 2 * HP * ROPE
WAF = wK + HP * KL
wV = 0
wO = wV + HP * KL
WMF = wO + HP * D


def fillers(it, s):
    pair, uu, qt = it * GP + s // 16, (s % 16) // 4, s % 4
    out = []
    if qt == 0 and UPI * it + s // 4 + 2 < NU:
        out.append(("q", UPI * it + s // 4 + 2))
    if uu == 0 and qt == 1 and pair + 1 < NP:
        out.append(("A", pair + 1))
    if s % 8 == 3 and OPI * it + s // 8 >= 1:
        out.append(("OT", OPI * it + s // 8 - 1))
    if s in OUT_STEPS and it >= 1:
        out.append(("out", NT * (it - 1) + OUT_STEPS.index(s)))
    if s in M_STEPS:
        out.append(("M", GP * it + M_STEPS.index(s)))
    return out


OUT_STEPS = [5, 6, 9, 10, 13, 14, 15, 18]
M_STEPS = [22, 26]
START = [("A", 0), ("q", 0), ("q", 1)]
DRAIN = [("OT", NO - 1)] + [("out", NT * (NI - 1) + t) for t in range(NT)]
RING = {}
for _item in START + [i for it in range(NI) for s in range(SPI) for i in fillers(it, s)] + DRAIN:
    RING[_item] = len(RING)
RPI = sum(len(fillers(1, s)) for s in range(SPI))


def W(it, value, rate):
    return value if isinstance(it, int) else it * rate + (value - rate)


def attention_kernel(nc, x, w1, wb, lbt, wp, qw, kvw, bb, cosq, sinq, cosk, sink, identd, maskd, identbd,
                     iotad, out):
    ctx = ExitStack()
    with ctx:
        def sb(name, shape, dt=f32):
            return ctx.enter_context(nc.sbuf_tensor(name, shape, dt))

        def sem(name):
            return ctx.enter_context(nc.semaphore(name))

        bank = [ctx.enter_context(nc.psum_tensor(f"bank{i}", [P, 512], f32)) for i in range(8)]
        sBank, tBank, oBank, rBank = bank[0:2], bank[2:4], bank[4:6], bank[6:8]

        ident = sb("ident", [P, P])
        identb = sb("identb", [P, P], bf16)
        mask = sb("mask", [P, P], bf16)
        CQ = sb("CQ", [P, S])
        SQ = sb("SQ", [P, S])
        CK = sb("CK", [P, NQ, ROPE])
        SK = sb("SK", [P, NQ, ROPE])
        qwb = sb("qwb", [P, QL])
        kvwb = sb("kvwb", [P, KL])
        kvcol = sb("kvcol", [P, 1])
        kvs = sb("kvs", [P, 1])
        bbb = sb("bbb", [P, D])
        iota = sb("iota", [P, NE])
        lbT = sb("lbT", [P, D])

        kTh, kTl = sb("kTh", [P, B * S], f32r), sb("kTl", [P, B * S], f32r)
        ch, cl = sb("ch", [P, NT, KL], f16), sb("cl", [P, NT, KL], f16)
        R1, R2, R3 = (sb(f"R{i}", [P, B * S], f32r) for i in (1, 2, 3))
        gate = sb("gate", [P, NT, D])
        Wbuf = sb("Wbuf", [P, 2 * (WAF + WMF)])
        WA = [Wbuf[:, i * WAF:(i + 1) * WAF] for i in range(2)]
        WM = [Wbuf[:, 2 * WAF + i * WMF:2 * WAF + (i + 1) * WMF] for i in range(2)]
        w1raw = Wbuf[:, 0:KD * C1].rearrange("p (k c) -> p k c", k=KD)
        wbraw = Wbuf[:, KD * D:2 * KD * D].rearrange("p (k c) -> p k c", k=KD)
        QWh = [sb(f"QWh{i}", [P, 2, HP, P], f32r) for i in range(2)]
        QWl = [sb(f"QWl{i}", [P, 2, HP, P], f32r) for i in range(2)]
        q32 = [sb(f"q32_{i}", [P, S]) for i in range(2)]
        qs = [sb(f"qs{i}", [P, S]) for i in range(2)]
        qh = [sb(f"qh{i}", [P, S], f32r) for i in range(4)]
        ql = [sb(f"ql{i}", [P, S], f32r) for i in range(4)]
        nmax = sb("nmax", [P, 8])
        sums = sb("sums", [P, 4, NQ * HP])
        rinv = sb("rinv", [P, 2, NQ * HP])

        s_x = [sem(f"x{t}") for t in range(NT)]
        s_const, s_w1d, s_wbd = sem("constants_loaded"), sem("w1_loaded"), sem("wb_loaded")
        s_wa = [sem(f"query_weights{i}_loaded") for i in range(2)]
        s_wm = [sem(f"merge_weights{i}_loaded") for i in range(2)]
        s_wh, s_wl = sem("weights_high"), sem("weights_low")
        s_dv, s_sq = sem("vector_chain"), sem("sqrt_done")
        s_rms = sem("rms_done")
        s_varq = sem("variance_ready")
        s_xn, s_xt, s_xh, s_xl = sem("xn_ready"), sem("xT_psum"), sem("xT_high"), sem("xT_low")
        s_pr, s_prc, s_ba, s_zb = sem("proj_psum"), sem("proj_copied"), sem("base_psum"), sem("base_added")
        s_ms = sem("mean_squares_ready")
        s_kq, s_qk, s_qkh, s_qkl = sem("kc_qn_ready"), sem("kcqn_psum"), sem("kcqn_high"), sem("kcqn_low")
        s_pool = sem("gpsimd_chain")
        s_ed, s_ex = sem("router_gap_ready"), sem("router_exp")
        s_hw, s_ht, s_htc = sem("lora_hidden_ready"), sem("lora_hiddenT_psum"), sem("lora_hiddenT_copied")
        s_lo, s_z, s_ez, s_g = sem("lora_psum"), sem("z_ready"), sem("exp_z"), sem("gate_ready")
        s_full, s_drained = sem("filler_psum"), sem("filler_drained")
        s_hi = sem("filler_high")
        s_wrh, s_wr = sem("rope_weights_high"), sem("rope_weights_split")
        s_qv, s_qa, s_qh, s_ql = sem("q_sin"), sem("q_roped"), sem("q_high"), sem("q_low")
        s_S, s_max, s_exp = sem("scores"), sem("row_max"), sem("row_exp")
        s_T, s_ph, s_pl = sem("probsT"), sem("probsT_high"), sem("probsT_low")
        s_PV, s_ri, s_o = sem("latent_out"), sem("row_sums_inverted"), sem("latent_out_normed")
        s_acc, s_acc0 = sem("acc_added"), sem("acc_zeroed")
        s_fin, s_fm, s_fx, s_xr, s_out = (sem("attn_out_final"), sem("gated"), sem("residual_added"),
                                          sem("x_reloaded"), sem("stored"))

        def dup(t):
            return t

        def unit_of(n):
            return n // NQ

        start_ctx = ExitStack()

        def st(name, shape, dt=f32):
            return start_ctx.enter_context(nc.sbuf_tensor(name, shape, dt))

        xin = [st(f"xin{i}", [P, D]) for i in range(4)]
        xn = [st(f"xn{i}", [P, D]) for i in range(2)]
        xTh = [st(f"xTh{i}", [P, KD, P], f32r) for i in range(3)]
        xTl = [st(f"xTl{i}", [P, KD, P], f32r) for i in range(3)]
        w1h, w1l = st("w1h", [P, KD, C1], f32r), st("w1l", [P, KD, C1], f32r)
        wbh, wbl = st("wbh", [P, KD, D], f32r), st("wbl", [P, KD, D], f32r)
        pr = st("pr", [P, NT, C1])
        qn = st("qn", [P, NT, 256])
        kc = st("kc", [P, NT, KL + ROPE])
        stats = st("stats", [P, NT, 6])
        mv = st("mv", [P, NT, 2])
        rstd = st("rstd", [P, NT])
        junk = st("junk", [P, QL])
        ms = st("ms", [P, NT, 2])
        cf = st("cf", [P, NT, KL])
        t2 = st("t2", [P, NT, ROPE])
        top = st("top", [P, NT, 8])
        topi = st("topi", [P, NT, 8], u32)
        idx = st("idx", [P, NT, 2])
        gap = st("gap", [P, NT])
        eg = st("eg", [P, NT])
        p12 = st("p12", [P, 2, NT])
        oh = st("oh", [P, 2, NT, NE])
        hw = st("hw", [P, NT, NE * R])
        hwT = st("hwT", [P, NT, P])
        ez = [st(f"ez{i}", [P, D]) for i in range(2)]
        start_ctx.close()
        Pr = [sb(f"probs{i}", [P, S]) for i in range(4)]
        Ph = [sb(f"probsTh{i}", [P, S], f16) for i in range(4)]
        Pl = [sb(f"probsTl{i}", [P, S], f16) for i in range(4)]
        osb = [sb(f"osb{i}", [P, NQ, P]) for i in range(2)]
        OTh, OTl = sb("OTh", [P, GP, B * S], f32r), sb("OTl", [P, GP, B * S], f32r)
        Mh, Ml = sb("Mh", [P, GP, D], f32r), sb("Ml", [P, GP, D], f32r)
        acc = sb("acc", [P, NT, D])

        block = ctx.enter_context(nc.Block())
        x_t = x.rearrange("b (q p) d -> p (b q) d", p=P)
        out_t = out.rearrange("b (q p) d -> p (b q) d", p=P)
        xres = [Wbuf[:, t * D:(t + 1) * D] for t in range(NT)]

        @block.sync
        def _(sp):
            for t in range(NT):
                if t >= 4:
                    sp.wait_ge(s_xn, t - 3)
                sp.dma_start(xin[t % 4][:, :], x_t[:, t, :]).then_inc(s_x[t], 16)
                if t == 1:
                    sp.dma_start(w1raw, w1).then_inc(s_w1d, 16)
                if t == 3:
                    sp.dma_start(wbraw, wb).then_inc(s_wbd, 16)
            def load(it, p, pair, which):
                if which == 0:
                    sp.dma_start(WA[p % 2], wp[pair, :, 0:WAF]).then_inc(s_wa[p % 2], 16)
                else:
                    sp.dma_start(WM[p % 2], wp[pair, :, WAF:WAF + WMF]).then_inc(s_wm[p % 2], 16)

            sp.wait_ge(s_wl, 1)
            load(0, 0, 0, 0)
            load(0, 1, 1, 0)
            sp.wait_ge(s_wl, 2)
            load(0, 0, 0, 1)
            load(0, 1, 1, 1)
            sp.wait_ge(s_drained, RING["A", 0] + 1)
            sp.wait_ge(s_wr, 1)
            load(0, 2, 2, 0)

            def loads(it, k):
                for j in range(GP):
                    p = GP * k + j + 1
                    if p + 2 < NP:
                        nxt = p + 2 if isinstance(it, int) else sp.snap(it * GP + (j + 3))
                        sp.wait_ge(s_drained, W(it, RING["A", p] + 1, RPI))
                        sp.wait_ge(s_wr, W(it, p + 1, GP))
                        load(it, p, nxt, 0)
                for j in range(GP):
                    p = GP * k + j
                    if p + 2 < NP:
                        nxt = p + 2 if isinstance(it, int) else sp.snap(it * GP + (j + 2))
                        sp.wait_ge(s_drained, W(it, RING["M", p] + 1, RPI))
                        load(it, p, nxt, 1)

            loads(0, 0)
            with sp.Fori(1, NI - 2) as i:
                loads(i, 1)
            loads(NI - 2, NI - 2)
            loads(NI - 1, NI - 1)
            sp.wait_ge(s_drained, RING["M", NP - 1] + 1)
            sp.dma_start(Wbuf[:, :].rearrange("p (t d) -> p t d", t=NT), x_t).then_inc(s_xr, 16)
            for t in range(NT):
                sp.wait_ge(s_fx, t + 1)
                sp.dma_start(out_t[:, t, :], acc[:, t, :]).then_inc(s_out, 16)
            sp.wait_ge(s_out, 16 * NT)

        @block.tensor
        def _(pe):
            pe.wait_ge(s_const, 16 * 15)
            three = ((0, 0), (0, 1), (1, 0))

            def x_transposes(t):
                pe.wait_ge(s_xn, t + 1)
                if t >= 2:
                    pe.wait_ge(s_xl, t - 1)
                for k in range(KD):
                    mm = pe.transpose(bank[t % 2][:, k * P:(k + 1) * P], xn[t % 2][:, k * P:(k + 1) * P], ident[:, :])
                mm.then_inc(s_xt, 1)

            def project(t):
                pe.wait_ge(s_xl, t + 1)
                if t == 0:
                    pe.wait_ge(s_wl, 1)
                if t >= 2:
                    pe.wait_ge(s_prc, t - 1)
                n = 0
                for k in range(KD):
                    for a, b in three:
                        mm = pe.matmul(bank[2 + t % 2][:, 0:C1], (xTh, xTl)[a][t % 3][:, k, :],
                                       (w1h, w1l)[b][:, k, :], start=(n == 0), stop=(n == 3 * KD - 1))
                        n += 1
                mm.then_inc(s_pr, 1)

            def base(t):
                if t == 0:
                    pe.wait_ge(s_wl, 2)
                if t >= 2:
                    pe.wait_ge(s_zb, t - 1)
                n = 0
                for k in range(KD):
                    for a, b in three:
                        mm = pe.matmul(bank[4 + t % 2][:, :], (xTh, xTl)[a][t % 3][:, k, :],
                                       (wbh, wbl)[b][:, k, :], start=(n == 0), stop=(n == 3 * KD - 1))
                        n += 1
                mm.then_inc(s_ba, 1)

            x_transposes(0)
            for t in range(NT):
                if t + 1 < NT:
                    x_transposes(t + 1)
                project(t)
                if t >= 1:
                    base(t - 1)
            base(NT - 1)

            def key_query_transposes(t):
                if t % NQ == 0:
                    pe.wait_ge(s_kq, t // NQ + 1)
                if t >= 2:
                    pe.wait_ge(s_qkl, t - 1)
                for j, src in enumerate((kc[:, t, :], qn[:, t, 0:P], qn[:, t, P:2 * P])):
                    mm = pe.transpose(bank[6 + t % 2][:, j * P:(j + 1) * P], src, ident[:, :])
                mm.then_inc(s_qk, 1)

            for t in range(NT):
                key_query_transposes(t)

            def ring_slot(it, item):
                r = RING[item]
                if r == 0:
                    pe.wait_ge(s_qkl, NT)
                if r >= 2:
                    pe.wait_ge(s_drained, W(it, r - 1, RPI))
                return rBank[r % 2]

            def absorb(it, p):
                dst = ring_slot(it, ("A", p))
                pe.wait_ge(s_wa[p % 2], W(it, 16 * (p // 2 + 1), 16 * GP // 2))
                w = WA[p % 2]
                for c in range(2):
                    for h in range(HP):
                        o = (c * HP + h) * KL
                        mm = pe.matmul(dst[:, o:o + KL], w[:, wQ + h * 256 + c * P:wQ + h * 256 + (c + 1) * P],
                                       w[:, wK + h * KL:wK + (h + 1) * KL], start=True, stop=True)
                mm.then_inc(s_full, 1)

            def query(it, u):
                p, b, h = u // 4, (u // 2) % 2, u % 2
                dst = ring_slot(it, ("q", u))
                if u % 4 == 0:
                    pe.wait_ge(s_drained, W(it, RING["A", p] + 1, RPI))
                    pe.wait_ge(s_wr, W(it, p + 1, GP))
                h_, l_ = QWh[p % 2], QWl[p % 2]
                cols = slice(b * S, (b + 1) * S)
                work = ((h_, 0, R1), (h_, 0, R2), (l_, 0, R1), (h_, 1, R3), (l_, 1, R3))
                for n, (w, c, r) in enumerate(work):
                    mm = pe.matmul(dst[:, :], w[:, c, h, :], r[:, cols], start=(n == 0), stop=(n == 4))
                mm.then_inc(s_full, 1)

            def merge(it, p):
                dst = ring_slot(it, ("M", p))
                pe.wait_ge(s_wm[p % 2], W(it, 16 * (p // 2 + 1), 16 * GP // 2))
                w = WM[p % 2]
                for h in range(HP):
                    mm = pe.matmul(dst[h * KL:(h + 1) * KL, :], w[:, wV + h * KL:wV + (h + 1) * KL],
                                   w[:, wO + h * D:wO + (h + 1) * D], start=True, stop=True)
                mm.then_inc(s_full, 1)

            def out_transposes(it, ob):
                dst = ring_slot(it, ("OT", ob))
                pe.wait_ge(s_o, W(it, ob + 1, OPI))
                for q in range(NQ):
                    mm = pe.transpose(dst[:, q * P:(q + 1) * P], osb[ob % 2][:, q, :], ident[:, :])
                mm.then_inc(s_full, 1)

            def out_project(it, ot):
                g, t = ot // NT, ot % NT
                dst = ring_slot(it, ("out", ot))
                if t == 0:
                    pe.wait_ge(s_drained, W(it, RING["OT", OPI * (g + 1) - 1] + 1, RPI))
                n = 0
                for j in range(GP):
                    for a, b in three:
                        mm = pe.matmul(dst[:, :], (OTh, OTl)[a][:, j, t * P:(t + 1) * P], (Mh, Ml)[b][:, j, :],
                                       start=(n == 0), stop=(n == 3 * GP - 1))
                        n += 1
                mm.then_inc(s_full, 1)

            fill = {"A": absorb, "q": query, "M": merge, "OT": out_transposes, "out": out_project}

            def scores(it, n):
                u, qt = unit_of(n), n % NQ
                b = (u // 2) % 2
                if qt == 0:
                    pe.wait_ge(s_ql, W(it, u + 1, UPI))
                w = (qt + 1) * P
                dst = sBank[n % 2]
                for m, (a, k) in enumerate(((qh, kTh), (qh, kTl), (ql, kTh))):
                    pe.matmul(dst[:, 0:w], a[u % 4][:, qt * P:(qt + 1) * P], k[:, b * S:b * S + w],
                              start=(m == 0), stop=False)
                pe.matmul(dst[:, w - P:w], identb[:, :], mask[:, :], start=False, stop=True).then_inc(s_S, 1)

            def transposes(it, n):
                pe.wait_ge(s_exp, W(it, n + 1, SPI))
                if n >= 2:
                    pe.wait_ge(s_pl, W(it, n - 1, SPI))
                for k in range(n % NQ + 1):
                    mm = pe.transpose(tBank[n % 2][:, k * P:(k + 1) * P], Pr[n % 4][:, k * P:(k + 1) * P], ident[:, :])
                mm.then_inc(s_T, 1)

            def times_latents(it, n):
                u, qt = unit_of(n), n % NQ
                b, h, ob = (u // 2) % 2, u % 2, u // 2
                pe.wait_ge(s_pl, W(it, n + 1, SPI))
                if h == 0 and qt == 0 and ob >= 2:
                    pe.wait_ge(s_o, W(it, ob - 1, OPI))
                dst = oBank[ob % 2][:, (qt * HP + h) * KL:(qt * HP + h + 1) * KL]
                m, last = 0, 3 * (qt + 1) - 1
                for k in range(qt + 1):
                    for a, c in ((Ph, ch), (Ph, cl), (Pl, ch)):
                        mm = pe.matmul(dst, a[n % 4][:, k * P:(k + 1) * P], c[:, b * NQ + k, :],
                                       start=(m == 0), stop=(m == last))
                        m += 1
                mm.then_inc(s_PV, 1)

            for kind, i in START:
                fill[kind](0, i)

            for g in range(2):
                pe.wait_ge(s_hw, 1)
                for j in range(4):
                    mm = pe.transpose(bank[g][:, j * P:(j + 1) * P], hw[:, 4 * g + j, :], ident[:, :])
                mm.then_inc(s_ht, 1)
            for t in range(NT):
                pe.wait_ge(s_htc, t // 4 + 1)
                if t == 0:
                    pe.wait_ge(s_prc, NT)
                    pe.wait_ge(s_zb, NT)
                if t >= 4:
                    pe.wait_ge(s_z, t - 3)
                pe.matmul(bank[2 + t % 4][:, :], hwT[:, t, :], lbT[:, :], start=True, stop=True).then_inc(s_lo, 1)

            pe.wait_ge(s_z, NT)
            pe.wait_ge(s_htc, 2)

            def step(it, k, s):
                n = SPI * k + s
                transposes(it, n)
                if n + 2 < NN:
                    scores(it, n + 2)
                for kind, i in fillers(k, s):
                    fill[kind](it, i)
                if n >= 2:
                    times_latents(it, n - 2)

            scores(0, 0)
            scores(0, 1)
            for s in range(SPI):
                step(0, 0, s)
            with pe.Fori(1, NI - 1) as i:
                for s in range(SPI):
                    step(i, 1, s)
            for s in range(SPI):
                step(NI - 1, NI - 1, s)
            times_latents(0, NN - 2)
            times_latents(0, NN - 1)
            for kind, i in DRAIN:
                fill[kind](0, i)

        @block.scalar
        def _(act):
            pairs = ((ident, identd), (identb, identbd), (mask, maskd), (CQ, cosq), (SQ, sinq), (CK, cosk),
                     (SK, sink), (iota, iotad), (lbT, lbt))
            for dst, src in pairs:
                act.dma_start(dst[:], src).then_inc(s_const, 16)
            act.dma_start(qwb[:, :], qw.partition_broadcast(P)).then_inc(s_const, 16)
            act.dma_start(kvwb[:, :], kvw.partition_broadcast(P)).then_inc(s_const, 16)
            act.dma_start(bbb[:, :], bb.partition_broadcast(P)).then_inc(s_const, 16)
            for h in range(HP):
                act.dma_start(kvcol[h * KL:(h + 1) * KL, :], kvw.rearrange("(c a) -> c a", a=1)).then_inc(s_const, 16)
            act.dma_start(junk[:, 0:NE], iotad).then_inc(s_const, 16)

            def high_x(t):
                act.wait_ge(s_xt, t + 1)
                act.activation(xTh[t % 3][:, :, :], bank[t % 2][:, :].rearrange("p (k t) -> p k t", k=KD),
                               ACT.Copy).then_inc(s_xh, 1)

            def copy_projection(t):
                act.wait_ge(s_pr, t + 1)
                act.activation(pr[:, t, :], bank[2 + t % 2][:, 0:C1], ACT.Copy).then_inc(s_prc, 1)

            def root(t):
                act.wait_ge(s_varq, t + 1)
                act.activation(rstd[:, t:t + 1], mv[:, t, 1:2], ACT.Sqrt).then_inc(s_sq, 1)

            root(0)
            act.wait_ge(s_w1d, 16)
            act.activation(w1h[:, :, :], w1raw, ACT.Copy).then_inc(s_wh, 1)
            root(1)
            high_x(0)
            act.wait_ge(s_wbd, 16)
            act.activation(wbh[:, :, :], wbraw, ACT.Copy).then_inc(s_wh, 1)
            for t in range(NT):
                if t + 2 < NT:
                    root(t + 2)
                if t + 1 < NT:
                    high_x(t + 1)
                copy_projection(t)
                if t % NQ == NQ - 1:
                    b = t // NQ
                    act.wait_ge(s_ms, b + 1)
                    act.activation(ms[:, b * NQ:(b + 1) * NQ, :], ms[:, b * NQ:(b + 1) * NQ, :], ACT.Sqrt)\
                       .then_inc(s_rms, 1)

            for t in range(NT):
                act.wait_ge(s_qk, t + 1)
                src = bank[6 + t % 2]
                for j, dst in enumerate((kTh, R1, R3)):
                    c = act.activation(dst[:, t * P:(t + 1) * P], src[:, j * P:(j + 1) * P], ACT.Copy)
                c.then_inc(s_qkh, 1)

            def high(it, item):
                kind, i = item
                r = RING[item]
                src = rBank[r % 2]
                if kind == "A":
                    act.wait_ge(s_full, W(it, r + 1, RPI))
                    act.activation(QWh[i % 2][:, :, :, 0:KL], src[:, 0:4 * KL].rearrange("p (c h k) -> p c h k", c=2, h=2),
                                   ACT.Copy).then_inc(s_hi, 1)
                    act.activation(QWh[i % 2][:, :, :, KL:P],
                                   WA[i % 2][:, wR:wR + 4 * ROPE].rearrange("p (c h k) -> p c h k", c=2, h=2),
                                   ACT.Copy).then_inc(s_wrh, 1)
                if kind == "M":
                    act.wait_ge(s_full, W(it, r + 1, RPI))
                    act.activation(Mh[:, i % GP, :], src[:, :], ACT.Identity, scale=kvs[:, 0:1]).then_inc(s_hi, 1)
                if kind == "OT":
                    act.wait_ge(s_full, W(it, r + 1, RPI))
                    act.activation(OTh[:, (i // B) % GP, (i % B) * S:(i % B + 1) * S], src[:, :], ACT.Copy).then_inc(s_hi, 1)

            def high_query(it, u):
                act.wait_ge(s_qa, W(it, u + 1, UPI))
                if u >= 4:
                    act.wait_ge(s_S, W(it, NQ * (u - 3), SPI))
                act.activation(qh[u % 4][:, :], q32[u % 2][:, :], ACT.Copy).then_inc(s_qh, 1)

            def exps(it, n):
                u, qt = unit_of(n), n % NQ
                w = (qt + 1) * P
                act.wait_ge(s_max, W(it, n + 1, SPI))
                act.activation(Pr[n % 4][:, 0:w], sBank[n % 2][:, 0:w], ACT.Exp, bias=nmax[:, n % 8:n % 8 + 1],
                               scale=1.0, accum_out=sums[:, (u // 2) % 4, qt * HP + u % 2:qt * HP + u % 2 + 1])\
                   .then_inc(s_exp, 1)

            def high_probs(it, n):
                w = (n % NQ + 1) * P
                act.wait_ge(s_T, W(it, n + 1, SPI))
                if n >= 4:
                    act.wait_ge(s_PV, W(it, n - 3, SPI))
                act.activation(Ph[n % 4][:, 0:w], tBank[n % 2][:, 0:w], ACT.Copy, scale=PS).then_inc(s_ph, 1)

            high(0, ("A", 0))
            high_query(0, 0)
            high_query(0, 1)
            act.wait_ge(s_ed, 1)
            act.activation(eg[:, :], gap[:, :], ACT.Exp).then_inc(s_ex, 1)
            for g in range(2):
                act.wait_ge(s_ht, g + 1)
                act.activation(hwT[:, 4 * g:4 * g + 4, :], bank[g][:, :].rearrange("p (t c) -> p t c", t=4), ACT.Copy)\
                   .then_inc(s_htc, 1)
            for t in range(NT):
                act.wait_ge(s_z, t + 1)
                if t >= 2:
                    act.wait_ge(s_g, t - 1)
                act.activation(ez[t % 2][:, :], gate[:, t, :], ACT.Exp, scale=-1.0).then_inc(s_ez, 1)

            def step(it, k, s):
                n = SPI * k + s
                high_probs(it, n)
                if n + 2 < NN:
                    exps(it, n + 2)
                for item in fillers(k, s):
                    if item[0] == "q":
                        high_query(it, item[1])
                    else:
                        high(it, item)

            act.wait_ge(s_g, NT)
            exps(0, 0)
            exps(0, 1)
            for s in range(SPI):
                step(0, 0, s)
            with act.Fori(1, NI - 1) as i:
                for s in range(SPI):
                    step(i, 1, s)
            for s in range(SPI):
                step(NI - 1, NI - 1, s)
            high(0, DRAIN[0])

        @block.gpsimd
        def _(pool):
            chain = [0]

            def link(ins):
                chain[0] += 1
                ins.then_inc(s_pool, 1)
                pool.wait_ge(s_pool, chain[0])

            pool.wait_ge(s_wh, 1)
            pool.tensor_tensor(w1l[:, :, :], w1raw,
                               w1h[:, :, :].bitcast(f32), ALU.subtract).then_inc(s_wl, 1)
            pool.wait_ge(s_wh, 2)
            pool.tensor_tensor(wbl[:, :, :], wbraw,
                               wbh[:, :, :].bitcast(f32), ALU.subtract).then_inc(s_wl, 1)

            def rope_weights(it, p):
                pool.wait_ge(s_wrh, W(it, p + 1, GP))
                raw = WA[p % 2][:, wR:wR + 4 * ROPE].rearrange("p (c h k) -> p c h k", c=2, h=2)
                hi, lo = QWh[p % 2][:, :, :, KL:P], QWl[p % 2][:, :, :, KL:P]
                pool.tensor_tensor(lo, raw, hi.bitcast(f32), ALU.subtract).then_inc(s_wr, 1)

            def rope(it, u):
                i = u % 2
                if u >= 1:
                    pool.wait_ge(s_ql, W(it, u, UPI))
                if u % 4 == 3 and u // 4 + 1 < NP or u == 0:
                    pool.wait_ge(s_wr, W(it, (u + 1) // 4 + 1, GP))
                if u == 2:
                    pool.wait_ge(s_acc0, 1)
                pool.wait_ge(s_drained, W(it, RING["q", u] + 1, RPI))
                pool.tensor_tensor(qs[i][KL:P, :], qs[i][KL:P, :], SQ[KL:P, :], ALU.mult).then_inc(s_qv, 1)
                pool.wait_ge(s_qv, W(it, u + 1, UPI))
                pool.tensor_tensor(q32[i][KL:P, :], q32[i][KL:P, :], qs[i][KL:P, :], ALU.add).then_inc(s_qa, 1)
                pool.wait_ge(s_qh, W(it, u + 1, UPI))
                pool.tensor_tensor(ql[u % 4][:, :], q32[i][:, :], qh[u % 4][:, :].bitcast(f32), ALU.subtract)\
                    .then_inc(s_ql, 1)

            rope_weights(0, 0)
            rope(0, 0)
            rope(0, 1)
            pool.wait_ge(s_g, NT)
            pool.memset(acc[:, :, :], 0.0).then_inc(s_acc0, 1)

            def step(it, k, s):
                for kind, i in fillers(k, s):
                    if kind == "A":
                        rope_weights(it, i)
                    if kind == "q":
                        rope(it, i)

            for s in range(SPI):
                step(0, 0, s)
            with pool.Fori(1, NI - 1) as i:
                for s in range(SPI):
                    step(i, 1, s)
            for s in range(SPI):
                step(NI - 1, NI - 1, s)
            for t in range(NT):
                if t == 0:
                    pool.wait_ge(s_xr, 16)
                pool.wait_ge(s_fm, t + 1)
                pool.tensor_tensor(acc[:, t, :], acc[:, t, :], xres[t], ALU.add).then_inc(s_fx, 1)

        @block.vector
        def _(dve):
            chain = [0]

            def link(ins):
                chain[0] += 1
                ins.then_inc(s_dv, 1)
                dve.wait_ge(s_dv, chain[0])

            def variance(t):
                dve.wait_ge(s_x[t], 16)
                link(dve.bn_stats(stats[:, t, :], xin[t % 4][:, :]))
                link(dve.bn_aggr(mv[:, t, :], stats[:, t, :]))
                dve.tensor_scalar(mv[:, t, 1:2], mv[:, t, 1:2], EPS_LN, None, ALU.add).then_inc(s_varq, 1)

            def normalise(t):
                dve.wait_ge(s_sq, t + 1)
                link(dve.reciprocal(rstd[:, t:t + 1], rstd[:, t:t + 1]))
                if t >= 2:
                    dve.wait_ge(s_xt, t - 1)
                dve.tensor_scalar(xn[t % 2][:, :], xin[t % 4][:, :], mv[:, t, 0:1], rstd[:, t:t + 1],
                                  ALU.subtract, ALU.mult).then_inc(s_xn, 1)

            def low_x(t):
                dve.wait_ge(s_xh, t + 1)
                dve.tensor_tensor(xTl[t % 3][:, :, :], bank[t % 2][:, :].rearrange("p (k t) -> p k t", k=KD),
                                  xTh[t % 3][:, :, :].bitcast(f32), ALU.subtract).then_inc(s_xl, 1)

            def take_base(t):
                dve.wait_ge(s_ba, t + 1)
                dve.tensor_tensor(gate[:, t, :], bank[4 + t % 2][:, :], bbb[:, :], ALU.add).then_inc(s_zb, 1)

            def squares(t):
                dve.wait_ge(s_prc, t + 1)
                dve.tensor_tensor_reduce(junk[:, :], pr[:, t, cQ:cQ + QL], pr[:, t, cQ:cQ + QL], 1.0 / QL, EPS_RMS,
                                         ALU.mult, ALU.add, ms[:, t, 0:1])
                link(dve.tensor_tensor_reduce(cf[:, t, :], pr[:, t, cC:cC + KL], pr[:, t, cC:cC + KL], 1.0 / KL, EPS_RMS,
                                              ALU.mult, ALU.add, ms[:, t, 1:2]))

            def latents(b):
                ts = slice(b * NQ, (b + 1) * NQ)
                dve.wait_ge(s_rms, b + 1)
                link(dve.reciprocal(ms[:, ts, :], ms[:, ts, :]))
                for t in range(b * NQ, (b + 1) * NQ):
                    dve.scalar_tensor_tensor(out=qn[:, t, 0:QL], in0=pr[:, t, cQ:cQ + QL], scalar=ms[:, t, 0:1],
                                             in1=qwb[:, :], op0=ALU.mult, op1=ALU.mult)
                    dve.tensor_scalar(cf[:, t, :], pr[:, t, cC:cC + KL], ms[:, t, 1:2], None, ALU.mult)
                xk = pr[:, ts, cK:cK + ROPE]
                link(dve.tensor_tensor(kc[:, ts, KL:], xk, CK[:, :, :], ALU.mult))
                dve.tensor_copy(qn[:, ts, QL:256], qn[:, ts, P:QL])
                dve.tensor_copy(ch[:, ts, :], cf[:, ts, :])
                xe = xk.rearrange("p t (j a) -> p t j a", a=2)
                se = SK[:, :, :].rearrange("p t (j a) -> p t j a", a=2)
                te = t2[:, ts, :].rearrange("p t (j a) -> p t j a", a=2)
                dve.tensor_tensor(te[:, :, :, 0], xe[:, :, :, 1], se[:, :, :, 0], ALU.mult)
                link(dve.tensor_tensor(te[:, :, :, 1], xe[:, :, :, 0], se[:, :, :, 1], ALU.mult))
                dve.tensor_tensor(kc[:, ts, KL:], kc[:, ts, KL:], t2[:, ts, :], ALU.add)
                dve.tensor_tensor(cl[:, ts, :], cf[:, ts, :], ch[:, ts, :], ALU.subtract)
                kw = kvwb[:, :].unsqueeze(1).to_broadcast([P, NQ, KL])
                link(dve.tensor_tensor(kc[:, ts, 0:KL], cf[:, ts, :], kw, ALU.mult))
                dve.tensor_scalar(kc[:, ts, 0:KL], kc[:, ts, 0:KL], float(NOPE + ROPE) ** -0.5, None, ALU.mult)\
                   .then_inc(s_kq, 1)

            dve.wait_ge(s_const, 16 * 15)
            dve.tensor_scalar(kvs[:, :], kvcol[:, :], 1.0 / PS, None, ALU.mult)
            variance(0)
            variance(1)
            normalise(0)
            variance(2)
            normalise(1)
            low_x(0)
            for t in range(NT):
                if t + 3 < NT:
                    variance(t + 3)
                if t + 2 < NT:
                    normalise(t + 2)
                if t + 1 < NT:
                    low_x(t + 1)
                if t >= 1:
                    take_base(t - 1)
                squares(t)
                if t % NQ == NQ - 1:
                    dve.tensor_copy(junk[:, 0:1], ms[:, t, 0:1]).then_inc(s_ms, 1)
            take_base(NT - 1)
            latents(0)
            latents(1)

            for t in range(NT):
                dve.wait_ge(s_qkh, t + 1)
                src = bank[6 + t % 2]
                c = slice(t * P, (t + 1) * P)
                dve.tensor_tensor(kTl[:, c], src[:, 0:P], kTh[:, c].bitcast(f32), ALU.subtract)
                dve.tensor_tensor(R2[:, c], src[:, P:2 * P], R1[:, c].bitcast(f32), ALU.subtract)
                dve.tensor_tensor(R3[KL:P, c], src[KL:P, 2 * P:3 * P], R3[KL:P, c].bitcast(f32), ALU.subtract)\
                   .then_inc(s_qkl, 1)

            def drain(it, item):
                kind, i = item
                r = RING[item]
                src = rBank[r % 2]
                if kind == "A":
                    dve.wait_ge(s_hi, W(it, HI[item] + 1, HPI))
                    dst = QWh[i % 2][:, :, :, 0:KL]
                    dve.tensor_tensor(QWl[i % 2][:, :, :, 0:KL], src[:, 0:4 * KL].rearrange("p (c h k) -> p c h k", c=2, h=2),
                                      dst.bitcast(f32), ALU.subtract).then_inc(s_drained, 1)
                if kind == "M":
                    dve.wait_ge(s_hi, W(it, HI[item] + 1, HPI))
                    dve.scalar_tensor_tensor(out=Ml[:, i % GP, :], in0=src[:, :], scalar=kvs[:, 0:1],
                                             in1=Mh[:, i % GP, :].bitcast(f32), op0=ALU.mult, op1=ALU.subtract)\
                       .then_inc(s_drained, 1)
                if kind == "OT":
                    dve.wait_ge(s_hi, W(it, HI[item] + 1, HPI))
                    j, c = (i // B) % GP, slice((i % B) * S, (i % B + 1) * S)
                    dve.tensor_tensor(OTl[:, j, c], src[:, :], OTh[:, j, c].bitcast(f32), ALU.subtract)\
                       .then_inc(s_drained, 1)
                if kind == "q":
                    dve.wait_ge(s_full, W(it, r + 1, RPI))
                    if i >= 2:
                        dve.wait_ge(s_ql, W(it, i - 1, UPI))
                    dve.tensor_tensor(q32[i % 2][:, :], src[:, :], CQ[:, :], ALU.mult)
                    dve.stream_shuffle(qs[i % 2][KL:P, :], src[KL:P, :], SWAP).then_inc(s_drained, 1)
                if kind == "out":
                    t = i % NT
                    dve.wait_ge(s_full, W(it, r + 1, RPI))
                    if i == 0 or not isinstance(it, int):
                        dve.wait_ge(s_acc0, 1)
                    ins = dve.tensor_tensor(acc[:, t, :], acc[:, t, :], src[:, :], ALU.add)
                    ins.then_inc(s_drained, 1)
                    if i >= NT * (NI - 1):
                        dve.wait_ge(s_drained, r + 1)
                        dve.tensor_tensor(acc[:, t, :], acc[:, t, :], gate[:, t, :], ALU.mult).then_inc(s_fm, 1)

            for item in START:
                drain(0, item)

            for t in range(NT):
                ins = dve.max(top[:, t, :], pr[:, t, cL:cL + NE])
            link(ins)
            for t in range(NT):
                ins = dve.max_index(topi[:, t, :], top[:, t, :], pr[:, t, cL:cL + NE])
            link(ins)
            dve.tensor_tensor(gap[:, :], top[:, :, 1], top[:, :, 0], ALU.subtract).then_inc(s_ed, 1)
            link(dve.tensor_copy(idx[:, :, :], topi[:, :, 0:2]))
            dve.wait_ge(s_ex, 1)
            link(dve.tensor_scalar(p12[:, 1, :], eg[:, :], 1.0, None, ALU.add))
            link(dve.reciprocal(p12[:, 0, :], p12[:, 1, :]))
            link(dve.tensor_tensor(p12[:, 1, :], eg[:, :], p12[:, 0, :], ALU.mult))
            for j in range(2):
                for t in range(NT):
                    ins = dve.tensor_scalar(oh[:, j, t, :], iota[:, :], idx[:, t, j:j + 1], p12[:, j, t:t + 1],
                                            ALU.is_equal, ALU.mult)
            link(ins)
            link(dve.tensor_tensor(oh[:, 0, :, :], oh[:, 0, :, :], oh[:, 1, :, :], ALU.add))
            for t in range(NT):
                ins = dve.scalar_tensor_tensor(out=hw[:, t, :].rearrange("p (e r) -> p e r", e=NE),
                                               in0=pr[:, t, cH:cH + NE * R].rearrange("p (e r) -> p e r", e=NE),
                                               scalar=LORA_SCALE,
                                               in1=oh[:, 0, t, :].unsqueeze(2).to_broadcast([P, NE, R]),
                                               op0=ALU.mult, op1=ALU.mult)
            ins.then_inc(s_hw, 1)
            for t in range(NT):
                dve.wait_ge(s_lo, t + 1)
                dve.tensor_tensor(gate[:, t, :], gate[:, t, :], bank[2 + t % 4][:, :], ALU.add).then_inc(s_z, 1)
            for t in range(NT):
                dve.wait_ge(s_ez, t + 1)
                e = ez[t % 2]
                link(dve.tensor_scalar(e[:, :], e[:, :], 1.0, None, ALU.add))
                link(dve.reciprocal(e[:, :], e[:, :]))
                dve.tensor_tensor(gate[:, t, :], gate[:, t, :], e[:, :], ALU.mult).then_inc(s_g, 1)

            def row_max(it, n):
                w = (n % NQ + 1) * P
                dve.wait_ge(s_S, W(it, n + 1, SPI))
                dve.tensor_reduce(nmax[:, n % 8:n % 8 + 1], sBank[n % 2][:, 0:w], AX.X, ALU.max, negate=True)\
                   .then_inc(s_max, 1)

            def low_probs(it, n):
                w = (n % NQ + 1) * P
                dve.wait_ge(s_ph, W(it, n + 1, SPI))
                dve.scalar_tensor_tensor(out=Pl[n % 4][:, 0:w], in0=tBank[n % 2][:, 0:w], scalar=PS,
                                         in1=Ph[n % 4][:, 0:w], op0=ALU.mult, op1=ALU.subtract).then_inc(s_pl, 1)

            def normalise_block(it, ob):
                dve.wait_ge(s_PV, W(it, NQ * HP * (ob + 1), SPI))
                dve.reciprocal(rinv[:, ob % 2, :], sums[:, ob % 4, :]).then_inc(s_ri, 1)
                dve.wait_ge(s_ri, W(it, ob + 1, OPI))
                dve.tensor_tensor(osb[ob % 2][:, :, :].rearrange("p q (h c) -> p (q h) c", h=HP),
                                  oBank[ob % 2][:, :].rearrange("p (m c) -> p m c", c=KL),
                                  rinv[:, ob % 2, :].unsqueeze(2).to_broadcast([P, NQ * HP, KL]), ALU.mult)\
                   .then_inc(s_o, 1)

            def step(it, k, s):
                n = SPI * k + s
                if n + 2 < NN:
                    row_max(it, n + 2)
                low_probs(it, n)
                if s % 8 == 2 and n > 8:
                    normalise_block(it, OPI * k + s // 8 - 1)
                for item in fillers(k, s):
                    drain(it, item)

            row_max(0, 0)
            row_max(0, 1)
            for s in range(SPI):
                step(0, 0, s)
            with dve.Fori(1, NI - 1) as i:
                for s in range(SPI):
                    step(i, 1, s)
            for s in range(SPI):
                step(NI - 1, NI - 1, s)
            normalise_block(0, NO - 1)
            for item in DRAIN:
                drain(0, item)


HI = {}
for _item in RING:
    if _item[0] in ("A", "M", "OT"):
        HI[_item] = len(HI)
HPI = 2 * GP + OPI

_OUTS = [((B, S, D), "float32")]


def _tables():
    import numpy as np
    freqs = (1.0 / 10000.0 ** (np.arange(0, ROPE, 2, dtype=np.float32) / np.float32(ROPE))).astype(np.float32)
    ang = np.outer(np.arange(S, dtype=np.float32), freqs).astype(np.float32)
    cos, sin = np.cos(ang).astype(np.float32), np.sin(ang).astype(np.float32)
    c2 = np.repeat(cos, 2, axis=1)
    s2 = np.stack([-sin, sin], axis=-1).reshape(S, ROPE)
    scale = np.float32(float(NOPE + ROPE) ** -0.5)
    cosq = np.concatenate([np.ones((KL, S), np.float32), c2.T], axis=0)
    sinq = np.concatenate([np.zeros((KL, S), np.float32), s2.T], axis=0)
    cosk = (c2 * scale).reshape(NQ, P, ROPE).transpose(1, 0, 2)
    sink = (s2 * scale).reshape(NQ, P, ROPE).transpose(1, 0, 2)
    mask = np.triu(np.full((P, P), MASKED, np.float32), 1)
    return cosq, sinq, cosk, sink, np.eye(P, dtype=np.float32), mask, np.tile(np.arange(NE, dtype=np.float32), (P, 1))


def kernel(**inputs):
    import numpy as np
    import ml_dtypes
    import concourse.bacc as _bacc
    from concourse.bass_utils import run_bass_kernel_spmd as _run

    a = {k.replace("L0_attn_", "").replace("L0_ffn_", ""): np.asarray(v) for k, v in inputs.items()}

    def by_rows(w):
        return w.reshape(KD, P, -1).transpose(1, 0, 2)

    w1 = by_rows(np.concatenate([a["wq_a"].T, a["wkv_a"].T, a["lora_A"].reshape(NE * R, D).T, a["W_router"].T], axis=1))
    wb = by_rows(a["W_base"].T)
    lbt = a["lora_B"].transpose(0, 2, 1).reshape(NE * R, D)
    wqb = a["wq_b"].reshape(NP, HP, NOPE + ROPE, QL)
    nope = wqb[:, :, :NOPE, :].transpose(0, 2, 1, 3)
    nope = np.concatenate([nope, nope[..., P:QL]], axis=-1).reshape(NP, P, HP * 256)
    rope = wqb[:, :, NOPE:, :].transpose(0, 3, 1, 2)
    rope = np.stack([rope[:, 0:P], np.concatenate([rope[:, P:QL], rope[:, P:QL]], axis=1)], axis=2)
    rope = rope.reshape(NP, P, 2 * HP * ROPE)
    wkv = a["wkv_b"].reshape(NP, HP, 2, P, KL).transpose(0, 3, 2, 1, 4).reshape(NP, P, 2 * HP * KL)
    wo = a["wo"].T.reshape(NP, HP, VD, D).transpose(0, 2, 1, 3).reshape(NP, P, HP * D)
    wp = np.concatenate([nope, rope, wkv, wo], axis=-1)
    cosq, sinq, cosk, sink, ident, mask, iota = _tables()
    arrays_in = [a["x"], w1, wb, lbt, wp, a["q_norm_w"], a["kv_norm_w"], a["b_base"], cosq, sinq, cosk, sink,
                 ident, mask.astype(ml_dtypes.bfloat16), ident.astype(ml_dtypes.bfloat16), iota]
    names = ["x", "w1", "wb", "lbt", "wp", "qw", "kvw", "bb", "cosq", "sinq", "cosk", "sink", "ident", "mask",
             "identb", "iota"]
    nc = _bacc.Bacc("TRN2", target_bir_lowering=False, num_devices=1)
    arrays, args = {}, []
    for name, v in zip(names, arrays_in):
        v = np.ascontiguousarray(v)
        arrays[f"in_{name}"] = v
        args.append(nc.dram_tensor(f"in_{name}", v.shape, mybir.dt.from_np(v.dtype), kind="ExternalInput").ap())
    args.append(nc.dram_tensor("out_0", _OUTS[0][0], f32, kind="ExternalOutput").ap())
    attention_kernel(nc, *args)
    r = _run(nc, [arrays], core_ids=[0])
    return r.results[0]["out_0"]
```

```python
import concourse.bass as bass
from concourse import mybir
from contextlib import ExitStack

f32 = mybir.dt.float32
f32r = mybir.dt.float32r
f16 = mybir.dt.float16
bf16 = mybir.dt.bfloat16
u32 = mybir.dt.uint32
ALU = mybir.AluOpType
ACT = mybir.ActivationFunctionType
AX = mybir.AxisListType

P = 128
B, S, D = 2, 512, 512
NT = B * S // P
KD = D // P
NH, NOPE, ROPE, VD = 32, 128, 64, 128
QL, KL = 192, 64
NE, R = 8, 16
EPS_LN, EPS_RMS = 1e-5, 1e-6
LORA_SCALE = 32.0 / 16.0
NQ = S // P
HP = 2
NP = NH // HP
GP = 2
NI = NP // GP
UPI = GP * B * HP
NU = NI * UPI
SPI = UPI * NQ
NN = NU * NQ
OPI = GP * B
NO = NI * OPI
C1 = QL + KL + ROPE + NE * R + NE
cQ, cC, cK, cH, cL = 0, QL, QL + KL, QL + KL + ROPE, QL + KL + ROPE + NE * R
PS = 1024.0
MASKED = -1e37
CONSTS = 13
SWAP = [i ^ 1 for i in range(32)]

wQ = 0
wR = wQ + HP * 256
wK = wR + 2 * HP * ROPE
WAF = wK + HP * KL
wV = 0
wO = wV + HP * KL
WMF = wO + HP * D


def fillers(it, s):
    pair, uu, qt = it * GP + s // 16, (s % 16) // 4, s % 4
    out = []
    if qt == 0 and UPI * it + s // 4 + 2 < NU:
        out.append(("q", UPI * it + s // 4 + 2))
    if uu == 0 and qt == 1 and pair + 1 < NP:
        out.append(("A", pair + 1))
    if s % 8 == 3 and OPI * it + s // 8 >= 1:
        out.append(("OT", OPI * it + s // 8 - 1))
    if s in (2, 3) and it == 0:
        out.append(("HT", s - 2))
    if s in OUT_STEPS:
        out.append(("out", NT * (it - 1) + OUT_STEPS.index(s)) if it else ("ffn", OUT_STEPS.index(s)))
    if s in M_STEPS:
        out.append(("M", GP * it + M_STEPS.index(s)))
    return out


OUT_STEPS = [5, 6, 9, 10, 13, 14, 15, 18]
M_STEPS = [22, 26]
START = [("A", 0), ("q", 0), ("q", 1)]
DRAIN = [("OT", NO - 1)] + [("out", NT * (NI - 1) + t) for t in range(NT)]
RING = {}
for _item in START + [i for it in range(NI) for s in range(SPI) for i in fillers(it, s)] + DRAIN:
    RING[_item] = len(RING)
RPI = sum(len(fillers(1, s)) for s in range(SPI))


def W(it, value, rate):
    return value if isinstance(it, int) else it * rate + (value - rate)


def attention_kernel(nc, x, w1, wb, lbt, wp, qw, kvw, bb, cosq, sinq, cosk, sink, identd, maskd, identbd,
                     iotad, out):
    ctx = ExitStack()
    with ctx:
        def sb(name, shape, dt=f32):
            return ctx.enter_context(nc.sbuf_tensor(name, shape, dt))

        def sem(name):
            return ctx.enter_context(nc.semaphore(name))

        bank = [ctx.enter_context(nc.psum_tensor(f"bank{i}", [P, 512], f32)) for i in range(8)]
        sBank, tBank, oBank, rBank = bank[0:2], bank[2:4], bank[4:6], bank[6:8]

        ident = sb("ident", [P, P])
        identb = sb("identb", [P, P], bf16)
        mask = sb("mask", [P, P], bf16)
        CQ = sb("CQ", [P, S])
        SQ = sb("SQ", [P, S])
        CK = sb("CK", [P, NQ, ROPE])
        SK = sb("SK", [P, NQ, ROPE])
        qwb = sb("qwb", [P, QL])
        kvwb = sb("kvwb", [P, KL])
        kvcol = sb("kvcol", [P, 1])
        kvs = sb("kvs", [P, 1])
        bbb = sb("bbb", [P, D])
        iota = sb("iota", [P, NE])
        lbT = sb("lbT", [P, D])

        kTh, kTl = sb("kTh", [P, B * S], f32r), sb("kTl", [P, B * S], f32r)
        ch, cl = sb("ch", [P, NT, KL], f16), sb("cl", [P, NT, KL], f16)
        R1, R2, R3 = (sb(f"R{i}", [P, B * S], f32r) for i in (1, 2, 3))
        gate = sb("gate", [P, NT, D])
        Wbuf = sb("Wbuf", [P, 2 * (WAF + WMF)])
        WA = [Wbuf[:, i * WAF:(i + 1) * WAF] for i in range(2)]
        WM = [Wbuf[:, 2 * WAF + i * WMF:2 * WAF + (i + 1) * WMF] for i in range(2)]
        with ExitStack() as early:
            wbh, wbl = (early.enter_context(nc.sbuf_tensor(n, [P, KD, D], f32r)) for n in ("wbh", "wbl"))
        acc = sb("acc", [P, NT, D])
        xTh, xTl = sb("xTh", [P, KD, B * S], f32r), sb("xTl", [P, KD, B * S], f32r)
        hwT = sb("hwT", [P, NT, P])
        w1raw = Wbuf[:, 0:KD * C1].rearrange("p (k c) -> p k c", k=KD)
        wbraw = Wbuf[:, KD * D:2 * KD * D].rearrange("p (k c) -> p k c", k=KD)
        QWh = [sb(f"QWh{i}", [P, 2, HP, P], f32r) for i in range(2)]
        QWl = [sb(f"QWl{i}", [P, 2, HP, P], f32r) for i in range(2)]
        q32 = [sb(f"q32_{i}", [P, S]) for i in range(2)]
        qs = [sb(f"qs{i}", [P, S]) for i in range(2)]
        nmax = sb("nmax", [P, 8])
        sums = sb("sums", [P, 4, NQ * HP])
        rinv = sb("rinv", [P, 2, NQ * HP])

        s_x = [sem(f"x{t}") for t in range(NT)]
        s_const, s_w1d, s_wbd = sem("constants_loaded"), sem("w1_loaded"), sem("wb_loaded")
        s_wa = [sem(f"query_weights{i}_loaded") for i in range(2)]
        s_wm = [sem(f"merge_weights{i}_loaded") for i in range(2)]
        s_wh, s_wl = sem("weights_high"), sem("weights_low")
        s_dv, s_sq = sem("vector_chain"), sem("sqrt_done")
        s_rms = sem("rms_done")
        s_varq = sem("variance_ready")
        s_xn, s_xt, s_xh, s_xl = sem("xn_ready"), sem("xT_psum"), sem("xT_high"), sem("xT_low")
        s_pr, s_prc = sem("proj_psum"), sem("proj_copied")
        s_id, s_cf, s_qn, s_qd, s_kc, s_ch = (sem("identity_loaded"), sem("latents_normed"), sem("qn_ready"),
                                              sem("qn_doubled"), sem("kc_ready"), sem("latents_high"))
        s_ms = sem("mean_squares_ready")
        s_qk, s_qkh, s_qkl = sem("kcqn_psum"), sem("kcqn_high"), sem("kcqn_low")
        s_pool = sem("gpsimd_chain")
        s_ed, s_ex = sem("router_gap_ready"), sem("router_exp")
        s_hw, s_wt = sem("lora_hidden_ready"), sem("expert_weights_ready")
        s_sig, s_g = sem("sigmoid_ready"), sem("gate_ready")
        s_full, s_drained = sem("filler_psum"), sem("filler_drained")
        s_hi = sem("filler_high")
        s_wrh, s_wr = sem("rope_weights_high"), sem("rope_weights_split")
        s_qv, s_qa, s_qh, s_ql = sem("q_sin"), sem("q_roped"), sem("q_high"), sem("q_low")
        s_S, s_max, s_exp = sem("scores"), sem("row_max"), sem("row_exp")
        s_T, s_ph, s_pl = sem("probsT"), sem("probsT_high"), sem("probsT_low")
        s_PV, s_ri, s_o = sem("latent_out"), sem("row_sums_inverted"), sem("latent_out_normed")
        s_acc, s_acc0 = sem("acc_added"), sem("acc_zeroed")
        s_fin, s_fm, s_fx, s_xr, s_out = (sem("attn_out_final"), sem("gated"), sem("residual_added"),
                                          sem("x_reloaded"), sem("stored"))

        def unit_of(n):
            return n // NQ

        start_ctx = ExitStack()

        def st(name, shape, dt=f32):
            return start_ctx.enter_context(nc.sbuf_tensor(name, shape, dt))

        w1h, w1l = st("w1h", [P, KD, C1], f32r), st("w1l", [P, KD, C1], f32r)
        xin = [st(f"xin{i}", [P, D]) for i in range(4)]
        xn = [st(f"xn{i}", [P, D]) for i in range(2)]
        pr = st("pr", [P, NT, C1])
        qn = st("qn", [P, NT, 256])
        kc = st("kc", [P, NT, KL + ROPE])
        stats = st("stats", [P, NT, 6])
        mv = st("mv", [P, NT, 2])
        rstd = st("rstd", [P, NT])
        ms = st("ms", [P, NT, 2])
        cf = st("cf", [P, NT, KL])
        t2 = st("t2", [P, NT, ROPE])
        top = st("top", [P, NT, 8])
        topi = st("topi", [P, NT, 8], u32)
        idx = st("idx", [P, NT, 2])
        gap = st("gap", [P, NT])
        eg = st("eg", [P, NT])
        p12 = st("p12", [P, 2, NT])
        oh = st("oh", [P, 2, NT, NE])
        kvw_s = st("kvw_s", [P, KL])
        hw = st("hw", [P, NT, NE * R])
        start_ctx.close()
        qh = [sb(f"qh{i}", [P, S], f32r) for i in range(4)]
        ql = [sb(f"ql{i}", [P, S], f32r) for i in range(4)]
        Pr = [sb(f"probs{i}", [P, S]) for i in range(4)]
        Ph = [sb(f"probsTh{i}", [P, S], f16) for i in range(4)]
        Pl = [sb(f"probsTl{i}", [P, S], f16) for i in range(4)]
        osb = [sb(f"osb{i}", [P, NQ, P]) for i in range(2)]
        OTh, OTl = sb("OTh", [P, GP, B * S], f32r), sb("OTl", [P, GP, B * S], f32r)
        Mh, Ml = sb("Mh", [P, GP, D], f32r), sb("Ml", [P, GP, D], f32r)

        block = ctx.enter_context(nc.Block())
        x_t = x.rearrange("b (q p) d -> p (b q) d", p=P)
        out_t = out.rearrange("b (q p) d -> p (b q) d", p=P)
        xres = [Wbuf[:, t * D:(t + 1) * D] for t in range(NT)]

        @block.sync
        def _(sp):
            for t in range(NT):
                if t >= 4:
                    sp.wait_ge(s_xn, t - 3)
                sp.dma_start(xin[t % 4][:, :], x_t[:, t, :]).then_inc(s_x[t], 16)
                if t == 1:
                    sp.dma_start(w1raw, w1).then_inc(s_w1d, 16)
                if t == 3:
                    sp.dma_start(wbraw, wb).then_inc(s_wbd, 16)
            def load(it, p, pair, which):
                if which == 0:
                    sp.dma_start(WA[p % 2], wp[pair, :, 0:WAF]).then_inc(s_wa[p % 2], 16)
                else:
                    sp.dma_start(WM[p % 2], wp[pair, :, WAF:WAF + WMF]).then_inc(s_wm[p % 2], 16)

            sp.wait_ge(s_wl, 1)
            load(0, 0, 0, 0)
            load(0, 1, 1, 0)
            sp.wait_ge(s_wl, 2)
            load(0, 0, 0, 1)
            load(0, 1, 1, 1)
            sp.wait_ge(s_drained, RING["A", 0] + 1)
            sp.wait_ge(s_wr, 1)
            load(0, 2, 2, 0)

            def loads(it, k):
                for j in range(GP):
                    p = GP * k + j + 1
                    if p + 2 < NP:
                        nxt = p + 2 if isinstance(it, int) else sp.snap(it * GP + (j + 3))
                        sp.wait_ge(s_drained, W(it, RING["A", p] + 1, RPI))
                        sp.wait_ge(s_wr, W(it, p + 1, GP))
                        load(it, p, nxt, 0)
                for j in range(GP):
                    p = GP * k + j
                    if p + 2 < NP:
                        nxt = p + 2 if isinstance(it, int) else sp.snap(it * GP + (j + 2))
                        sp.wait_ge(s_drained, W(it, RING["M", p] + 1, RPI))
                        load(it, p, nxt, 1)

            loads(0, 0)
            with sp.Fori(1, NI - 2) as i:
                loads(i, 1)
            loads(NI - 2, NI - 2)
            loads(NI - 1, NI - 1)
            sp.wait_ge(s_drained, RING["M", NP - 1] + 1)
            sp.dma_start(Wbuf[:, :].rearrange("p (t d) -> p t d", t=NT), x_t).then_inc(s_xr, 16)
            for t in range(NT):
                sp.wait_ge(s_fx, t + 1)
                sp.dma_start(out_t[:, t, :], acc[:, t, :]).then_inc(s_out, 16)
            sp.wait_ge(s_out, 16 * NT)

        @block.tensor
        def _(pe):
            pe.wait_ge(s_id, 16)
            three = ((0, 0), (0, 1), (1, 0))

            def x_transposes(t):
                pe.wait_ge(s_xn, t + 1)
                if t >= 2:
                    pe.wait_ge(s_xl, t - 1)
                for k in range(KD):
                    mm = pe.transpose(bank[t % 2][:, k * P:(k + 1) * P], xn[t % 2][:, k * P:(k + 1) * P], ident[:, :])
                mm.then_inc(s_xt, 1)

            def project(t):
                pe.wait_ge(s_xl, t + 1)
                if t == 0:
                    pe.wait_ge(s_wl, 1)
                if t >= 2:
                    pe.wait_ge(s_prc, t - 1)
                n, tok = 0, slice(t * P, (t + 1) * P)
                for k in range(KD):
                    for a, b in three:
                        mm = pe.matmul(bank[2 + t % 2][:, 0:C1], (xTh, xTl)[a][:, k, tok],
                                       (w1h, w1l)[b][:, k, :], start=(n == 0), stop=(n == 3 * KD - 1))
                        n += 1
                mm.then_inc(s_pr, 1)

            def key_query_transposes(t):
                if t % NQ == 0:
                    b = t // NQ
                    pe.wait_ge(s_kc, b + 1)
                    pe.wait_ge(s_qn, b + 1)
                    pe.wait_ge(s_qd, b + 1)
                if t >= 2:
                    pe.wait_ge(s_qkl, t - 1)
                for j, src in enumerate((kc[:, t, :], qn[:, t, 0:P], qn[:, t, P:2 * P])):
                    mm = pe.transpose(bank[4 + t % 2][:, j * P:(j + 1) * P], src, ident[:, :])
                mm.then_inc(s_qk, 1)

            x_transposes(0)
            for t in range(NT):
                if t + 1 < NT:
                    x_transposes(t + 1)
                project(t)

            def ring_slot(it, item):
                r = RING[item]
                if r >= 2:
                    pe.wait_ge(s_drained, W(it, r - 1, RPI))
                return rBank[r % 2]

            def absorb(it, p):
                dst = ring_slot(it, ("A", p))
                pe.wait_ge(s_wa[p % 2], W(it, 16 * (p // 2 + 1), 16 * GP // 2))
                w = WA[p % 2]
                for c in range(2):
                    for h in range(HP):
                        o = (c * HP + h) * KL
                        mm = pe.matmul(dst[:, o:o + KL], w[:, wQ + h * 256 + c * P:wQ + h * 256 + (c + 1) * P],
                                       w[:, wK + h * KL:wK + (h + 1) * KL], start=True, stop=True)
                mm.then_inc(s_full, 1)

            def query(it, u):
                p, b, h = u // 4, (u // 2) % 2, u % 2
                dst = ring_slot(it, ("q", u))
                if u % 4 == 0:
                    pe.wait_ge(s_drained, W(it, RING["A", p] + 1, RPI))
                    pe.wait_ge(s_wr, W(it, p + 1, GP))
                h_, l_ = QWh[p % 2], QWl[p % 2]
                cols = slice(b * S, (b + 1) * S)
                work = ((h_, 0, R1), (h_, 0, R2), (l_, 0, R1), (h_, 1, R3), (l_, 1, R3))
                for n, (w, c, r) in enumerate(work):
                    mm = pe.matmul(dst[:, :], w[:, c, h, :], r[:, cols], start=(n == 0), stop=(n == 4))
                mm.then_inc(s_full, 1)

            def merge(it, p):
                dst = ring_slot(it, ("M", p))
                pe.wait_ge(s_wm[p % 2], W(it, 16 * (p // 2 + 1), 16 * GP // 2))
                w = WM[p % 2]
                for h in range(HP):
                    mm = pe.matmul(dst[h * KL:(h + 1) * KL, :], w[:, wV + h * KL:wV + (h + 1) * KL],
                                   w[:, wO + h * D:wO + (h + 1) * D], start=True, stop=True)
                mm.then_inc(s_full, 1)

            def out_transposes(it, ob):
                dst = ring_slot(it, ("OT", ob))
                pe.wait_ge(s_o, W(it, ob + 1, OPI))
                for q in range(NQ):
                    mm = pe.transpose(dst[:, q * P:(q + 1) * P], osb[ob % 2][:, q, :], ident[:, :])
                mm.then_inc(s_full, 1)

            def out_project(it, ot):
                g, t = ot // NT, ot % NT
                dst = ring_slot(it, ("out", ot))
                if t == 0:
                    pe.wait_ge(s_drained, W(it, RING["OT", OPI * (g + 1) - 1] + 1, RPI))
                n = 0
                for j in range(GP):
                    for a, b in three:
                        mm = pe.matmul(dst[:, :], (OTh, OTl)[a][:, j, t * P:(t + 1) * P], (Mh, Ml)[b][:, j, :],
                                       start=(n == 0), stop=(n == 3 * GP - 1))
                        n += 1
                mm.then_inc(s_full, 1)

            def lora_transposes(it, g):
                dst = ring_slot(it, ("HT", g))
                pe.wait_ge(s_hw, 1)
                for j in range(4):
                    mm = pe.transpose(dst[:, j * P:(j + 1) * P], hw[:, 4 * g + j, :], ident[:, :])
                mm.then_inc(s_full, 1)

            def linear(it, t):
                dst = ring_slot(it, ("ffn", t))
                if t == 0:
                    pe.wait_ge(s_wl, 2)
                    pe.wait_ge(s_drained, RING["HT", 1] + 1)
                n, tok = 0, slice(t * P, (t + 1) * P)
                for k in range(KD):
                    for a, b in three:
                        pe.matmul(dst[:, :], (xTh, xTl)[a][:, k, tok], (wbh, wbl)[b][:, k, :],
                                  start=(n == 0), stop=False)
                        n += 1
                pe.matmul(dst[:, :], hwT[:, t, :], lbT[:, :], start=False, stop=True).then_inc(s_full, 1)

            fill = {"HT": lora_transposes, "ffn": linear, "A": absorb, "q": query, "M": merge, "OT": out_transposes, "out": out_project}

            def scores(it, n):
                u, qt = unit_of(n), n % NQ
                b = (u // 2) % 2
                if qt == 0:
                    pe.wait_ge(s_ql, W(it, u + 1, UPI))
                w = (qt + 1) * P
                dst = sBank[n % 2]
                for m, (a, k) in enumerate(((qh, kTh), (qh, kTl), (ql, kTh))):
                    pe.matmul(dst[:, 0:w], a[u % 4][:, qt * P:(qt + 1) * P], k[:, b * S:b * S + w],
                              start=(m == 0), stop=False)
                pe.matmul(dst[:, w - P:w], identb[:, :], mask[:, :], start=False, stop=True).then_inc(s_S, 1)

            def transposes(it, n):
                pe.wait_ge(s_exp, W(it, n + 1, SPI))
                if n >= 2:
                    pe.wait_ge(s_pl, W(it, n - 1, SPI))
                for k in range(n % NQ + 1):
                    mm = pe.transpose(tBank[n % 2][:, k * P:(k + 1) * P], Pr[n % 4][:, k * P:(k + 1) * P], ident[:, :])
                mm.then_inc(s_T, 1)

            def times_latents(it, n):
                u, qt = unit_of(n), n % NQ
                b, h, ob = (u // 2) % 2, u % 2, u // 2
                pe.wait_ge(s_pl, W(it, n + 1, SPI))
                if h == 0 and qt == 0 and ob >= 2:
                    pe.wait_ge(s_o, W(it, ob - 1, OPI))
                dst = oBank[ob % 2][:, (qt * HP + h) * KL:(qt * HP + h + 1) * KL]
                m, last = 0, 3 * (qt + 1) - 1
                for k in range(qt + 1):
                    for a, c in ((Ph, ch), (Ph, cl), (Pl, ch)):
                        mm = pe.matmul(dst, a[n % 4][:, k * P:(k + 1) * P], c[:, b * NQ + k, :],
                                       start=(m == 0), stop=(m == last))
                        m += 1
                mm.then_inc(s_PV, 1)

            for t in range(NQ):
                key_query_transposes(t)
            for kind, i in START:
                fill[kind](0, i)
            for t in range(NQ, NT):
                key_query_transposes(t)

            def step(it, k, s):
                n = SPI * k + s
                transposes(it, n)
                if n + 2 < NN:
                    scores(it, n + 2)
                for kind, i in fillers(k, s):
                    fill[kind](it, i)
                if n >= 2:
                    times_latents(it, n - 2)

            pe.wait_ge(s_xl, NT)
            pe.wait_ge(s_prc, NT)
            pe.wait_ge(s_qkl, NT)
            scores(0, 0)
            scores(0, 1)
            for s in range(SPI):
                step(0, 0, s)
            with pe.Fori(1, NI - 1) as i:
                for s in range(SPI):
                    step(i, 1, s)
            for s in range(SPI):
                step(NI - 1, NI - 1, s)
            times_latents(0, NN - 2)
            times_latents(0, NN - 1)
            for kind, i in DRAIN:
                fill[kind](0, i)

        @block.scalar
        def _(act):
            pairs = ((ident, identd), (identb, identbd), (mask, maskd), (CQ, cosq), (SQ, sinq), (CK, cosk),
                     (SK, sink), (iota, iotad), (lbT, lbt))
            for dst, src in pairs:
                act.dma_start(dst[:], src).then_inc(s_id if dst is ident else s_const, 16)
            act.dma_start(qwb[:, :], qw.partition_broadcast(P)).then_inc(s_const, 16)
            act.dma_start(kvwb[:, :], kvw.partition_broadcast(P)).then_inc(s_const, 16)
            act.dma_start(bbb[:, :], bb.partition_broadcast(P)).then_inc(s_const, 16)
            for h in range(HP):
                act.dma_start(kvcol[h * KL:(h + 1) * KL, :], kvw.rearrange("(c a) -> c a", a=1)).then_inc(s_const, 16)

            def high_x(t):
                act.wait_ge(s_xt, t + 1)
                act.activation(xTh[:, :, t * P:(t + 1) * P], bank[t % 2][:, :].rearrange("p (k t) -> p k t", k=KD),
                               ACT.Copy).then_inc(s_xh, 1)

            def copy_projection(t):
                act.wait_ge(s_pr, t + 1)
                act.activation(pr[:, t, :], bank[2 + t % 2][:, 0:C1], ACT.Copy).then_inc(s_prc, 1)

            def root(t):
                act.wait_ge(s_varq, t + 1)
                act.activation(rstd[:, t:t + 1], mv[:, t, 1:2], ACT.Sqrt).then_inc(s_sq, 1)

            root(0)
            act.wait_ge(s_w1d, 16)
            act.activation(w1h[:, :, :], w1raw, ACT.Copy).then_inc(s_wh, 1)
            root(1)
            high_x(0)
            act.wait_ge(s_wbd, 16)
            act.activation(wbh[:, :, :], wbraw, ACT.Copy).then_inc(s_wh, 1)
            def copies(b):
                ts = slice(b * NQ, (b + 1) * NQ)
                act.wait_ge(s_cf, b + 1)
                act.activation(ch[:, ts, :], cf[:, ts, :], ACT.Copy).then_inc(s_ch, 1)
                act.wait_ge(s_qn, b + 1)
                act.activation(qn[:, ts, QL:256], qn[:, ts, P:QL], ACT.Copy).then_inc(s_qd, 1)

            for t in range(NT):
                if t + 2 < NT:
                    root(t + 2)
                if t + 1 < NT:
                    high_x(t + 1)
                copy_projection(t)
                if t == NT - 3:
                    copies(0)
                if t % NQ == NQ - 1:
                    b = t // NQ
                    act.wait_ge(s_ms, b + 1)
                    act.activation(ms[:, b * NQ:(b + 1) * NQ, :], ms[:, b * NQ:(b + 1) * NQ, :], ACT.Sqrt)\
                       .then_inc(s_rms, 1)

            def high_kq(t):
                act.wait_ge(s_qk, t + 1)
                src = bank[4 + t % 2]
                for j, dst in enumerate((kTh, R1, R3)):
                    c = act.activation(dst[:, t * P:(t + 1) * P], src[:, j * P:(j + 1) * P], ACT.Copy)
                c.then_inc(s_qkh, 1)

            def high(it, item):
                kind, i = item
                r = RING[item]
                src = rBank[r % 2]
                if kind == "A":
                    act.wait_ge(s_full, W(it, r + 1, RPI))
                    act.activation(QWh[i % 2][:, :, :, 0:KL], src[:, 0:4 * KL].rearrange("p (c h k) -> p c h k", c=2, h=2),
                                   ACT.Copy).then_inc(s_hi, 1)
                    act.activation(QWh[i % 2][:, :, :, KL:P],
                                   WA[i % 2][:, wR:wR + 4 * ROPE].rearrange("p (c h k) -> p c h k", c=2, h=2),
                                   ACT.Copy).then_inc(s_wrh, 1)
                if kind == "M":
                    act.wait_ge(s_full, W(it, r + 1, RPI))
                    act.activation(Mh[:, i % GP, :], src[:, :], ACT.Identity, scale=kvs[:, 0:1]).then_inc(s_hi, 1)
                if kind == "OT":
                    act.wait_ge(s_full, W(it, r + 1, RPI))
                    act.activation(OTh[:, (i // B) % GP, (i % B) * S:(i % B + 1) * S], src[:, :], ACT.Copy).then_inc(s_hi, 1)

            def high_query(it, u):
                act.wait_ge(s_qa, W(it, u + 1, UPI))
                if u >= 4:
                    act.wait_ge(s_S, W(it, NQ * (u - 3), SPI))
                act.activation(qh[u % 4][:, :], q32[u % 2][:, :], ACT.Copy).then_inc(s_qh, 1)

            def exps(it, n):
                u, qt = unit_of(n), n % NQ
                w = (qt + 1) * P
                act.wait_ge(s_max, W(it, n + 1, SPI))
                act.activation(Pr[n % 4][:, 0:w], sBank[n % 2][:, 0:w], ACT.Exp, bias=nmax[:, n % 8:n % 8 + 1],
                               scale=1.0, accum_out=sums[:, (u // 2) % 4, qt * HP + u % 2:qt * HP + u % 2 + 1])\
                   .then_inc(s_exp, 1)

            def high_probs(it, n):
                w = (n % NQ + 1) * P
                act.wait_ge(s_T, W(it, n + 1, SPI))
                if n >= 4:
                    act.wait_ge(s_PV, W(it, n - 3, SPI))
                act.activation(Ph[n % 4][:, 0:w], tBank[n % 2][:, 0:w], ACT.Copy, scale=PS).then_inc(s_ph, 1)

            for t in range(NQ):
                high_kq(t)
            high(0, ("A", 0))
            copies(1)
            high_query(0, 0)
            for t in range(NQ, NT):
                high_kq(t)
            high_query(0, 1)
            act.wait_ge(s_ed, 1)
            act.activation(eg[:, :], gap[:, :], ACT.Exp).then_inc(s_ex, 1)

            def step(it, k, s):
                n = SPI * k + s
                high_probs(it, n)
                if n + 2 < NN:
                    exps(it, n + 2)
                for item in fillers(k, s):
                    high(it, item)
                if s % 4 == 2 and UPI * k + s // 4 + 2 < NU:
                    high_query(it, UPI * k + s // 4 + 2)

            act.wait_ge(s_hw, 1)
            exps(0, 0)
            exps(0, 1)
            for s in range(SPI):
                step(0, 0, s)
            with act.Fori(1, NI - 1) as i:
                for s in range(SPI):
                    step(i, 1, s)
            for s in range(SPI):
                step(NI - 1, NI - 1, s)
            high(0, DRAIN[0])
            for t in range(NT):
                if t >= 4:
                    act.wait_ge(s_g, t - 3)
                act.activation(Pr[t % 4][:, :], gate[:, t, :], ACT.Sigmoid).then_inc(s_sig, 1)

        @block.gpsimd
        def _(pool):
            chain = [0]

            def link(ins):
                chain[0] += 1
                ins.then_inc(s_pool, 1)
                pool.wait_ge(s_pool, chain[0])

            pool.wait_ge(s_wh, 1)
            pool.tensor_tensor(w1l[:, :, :], w1raw,
                               w1h[:, :, :].bitcast(f32), ALU.subtract).then_inc(s_wl, 1)
            pool.wait_ge(s_wh, 2)
            pool.tensor_tensor(wbl[:, :, :], wbraw,
                               wbh[:, :, :].bitcast(f32), ALU.subtract).then_inc(s_wl, 1)

            def rope_weights(it, p):
                pool.wait_ge(s_wrh, W(it, p + 1, GP))
                raw = WA[p % 2][:, wR:wR + 4 * ROPE].rearrange("p (c h k) -> p c h k", c=2, h=2)
                hi, lo = QWh[p % 2][:, :, :, KL:P], QWl[p % 2][:, :, :, KL:P]
                pool.tensor_tensor(lo, raw, hi.bitcast(f32), ALU.subtract).then_inc(s_wr, 1)

            def rope(it, u):
                i = u % 2
                if u >= 1:
                    pool.wait_ge(s_ql, W(it, u, UPI))
                if u % 4 == 3 and u // 4 + 1 < NP or u == 0:
                    pool.wait_ge(s_wr, W(it, (u + 1) // 4 + 1, GP))
                if u == 2:
                    pool.wait_ge(s_hw, 1)
                if u == UPI + 2:
                    pool.wait_ge(s_acc0, 1)
                pool.wait_ge(s_drained, W(it, RING["q", u] + 1, RPI))
                pool.tensor_tensor(qs[i][KL:P, :], qs[i][KL:P, :], SQ[KL:P, :], ALU.mult).then_inc(s_qv, 1)
                pool.wait_ge(s_qv, W(it, u + 1, UPI))
                pool.tensor_tensor(q32[i][KL:P, :], q32[i][KL:P, :], qs[i][KL:P, :], ALU.add).then_inc(s_qa, 1)
                pool.wait_ge(s_qh, W(it, u + 1, UPI))
                pool.tensor_tensor(ql[u % 4][:, :], q32[i][:, :], qh[u % 4][:, :].bitcast(f32), ALU.subtract)\
                    .then_inc(s_ql, 1)

            def keys(b):
                ts = slice(b * NQ, (b + 1) * NQ)
                pool.wait_ge(s_prc, (b + 1) * NQ)
                xk = pr[:, ts, cK:cK + ROPE]
                xe = xk.rearrange("p t (j a) -> p t j a", a=2)
                se = SK[:, :, :].rearrange("p t (j a) -> p t j a", a=2)
                te = t2[:, ts, :].rearrange("p t (j a) -> p t j a", a=2)
                pool.tensor_tensor(kc[:, ts, KL:], xk, CK[:, :, :], ALU.mult)
                pool.tensor_tensor(te[:, :, :, 0], xe[:, :, :, 1], se[:, :, :, 0], ALU.mult)
                link(pool.tensor_tensor(te[:, :, :, 1], xe[:, :, :, 0], se[:, :, :, 1], ALU.mult))
                pool.tensor_tensor(kc[:, ts, KL:], kc[:, ts, KL:], t2[:, ts, :], ALU.add)
                pool.wait_ge(s_cf, b + 1)
                pool.tensor_tensor(kc[:, ts, 0:KL], cf[:, ts, :], kvw_s[:, :].unsqueeze(1).to_broadcast([P, NQ, KL]),
                                   ALU.mult).then_inc(s_kc, 1)
                pool.wait_ge(s_ch, b + 1)
                link(pool.tensor_tensor(cl[:, ts, :], cf[:, ts, :], ch[:, ts, :], ALU.subtract))

            pool.wait_ge(s_const, 16 * CONSTS)
            link(pool.tensor_scalar(kvw_s[:, :], kvwb[:, :], float(NOPE + ROPE) ** -0.5, 1.0, ALU.mult, ALU.mult))
            keys(0)
            keys(1)
            rope_weights(0, 0)
            rope(0, 0)
            rope(0, 1)
            pool.wait_ge(s_wt, 1)
            pool.tensor_tensor(hw[:, :, :].rearrange("p t (e r) -> p (t e) r", e=NE),
                               pr[:, :, cH:cH + NE * R].rearrange("p t (e r) -> p t e r", e=NE),
                               oh[:, 0, :, :].unsqueeze(3).to_broadcast([P, NT, NE, R]), ALU.mult).then_inc(s_hw, 1)


            def step(it, k, s):
                for kind, i in fillers(k, s):
                    if kind == "A":
                        rope_weights(it, i)
                    if kind == "q":
                        rope(it, i)

            for s in range(SPI):
                step(0, 0, s)
            pool.wait_ge(s_full, RING["ffn", NT - 1] + 1)
            pool.memset(acc[:, :, :], 0.0).then_inc(s_acc0, 1)
            with pool.Fori(1, NI - 1) as i:
                for s in range(SPI):
                    step(i, 1, s)
            for s in range(SPI):
                step(NI - 1, NI - 1, s)
            for t in range(NT):
                pool.wait_ge(s_sig, t + 1)
                pool.tensor_tensor(gate[:, t, :], gate[:, t, :], Pr[t % 4][:, :], ALU.mult).then_inc(s_g, 1)
            for t in range(NT):
                if t == 0:
                    pool.wait_ge(s_xr, 16)
                pool.wait_ge(s_fm, t + 1)
                pool.tensor_tensor(acc[:, t, :], acc[:, t, :], xres[t], ALU.add).then_inc(s_fx, 1)

        @block.vector
        def _(dve):
            chain = [0]

            def link(ins):
                chain[0] += 1
                ins.then_inc(s_dv, 1)
                dve.wait_ge(s_dv, chain[0])

            def variance(t):
                dve.wait_ge(s_x[t], 16)
                link(dve.bn_stats(stats[:, t, :], xin[t % 4][:, :]))
                link(dve.bn_aggr(mv[:, t, :], stats[:, t, :]))
                dve.tensor_scalar(mv[:, t, 1:2], mv[:, t, 1:2], EPS_LN, None, ALU.add).then_inc(s_varq, 1)

            def normalise(t):
                dve.wait_ge(s_sq, t + 1)
                link(dve.reciprocal(rstd[:, t:t + 1], rstd[:, t:t + 1]))
                if t >= 2:
                    dve.wait_ge(s_xt, t - 1)
                dve.tensor_scalar(xn[t % 2][:, :], xin[t % 4][:, :], mv[:, t, 0:1], rstd[:, t:t + 1],
                                  ALU.subtract, ALU.mult).then_inc(s_xn, 1)

            def low_x(t):
                dve.wait_ge(s_xh, t + 1)
                tok = slice(t * P, (t + 1) * P)
                dve.tensor_tensor(xTl[:, :, tok], bank[t % 2][:, :].rearrange("p (k t) -> p k t", k=KD),
                                  xTh[:, :, tok].bitcast(f32), ALU.subtract).then_inc(s_xl, 1)

            def squares(t):
                dve.wait_ge(s_prc, t + 1)
                dve.tensor_tensor_reduce(qn[:, t, 0:QL], pr[:, t, cQ:cQ + QL], pr[:, t, cQ:cQ + QL], 1.0 / QL, EPS_RMS,
                                         ALU.mult, ALU.add, ms[:, t, 0:1])
                ins = dve.tensor_tensor_reduce(cf[:, t, :], pr[:, t, cC:cC + KL], pr[:, t, cC:cC + KL], 1.0 / KL, EPS_RMS,
                                               ALU.mult, ALU.add, ms[:, t, 1:2])
                if t % NQ == NQ - 1:
                    ins.then_inc(s_ms, 1)

            def latents(b):
                ts = slice(b * NQ, (b + 1) * NQ)
                dve.wait_ge(s_rms, b + 1)
                link(dve.reciprocal(ms[:, ts, :], ms[:, ts, :]))
                for t in range(b * NQ, (b + 1) * NQ):
                    ins = dve.tensor_scalar(cf[:, t, :], pr[:, t, cC:cC + KL], ms[:, t, 1:2], None, ALU.mult)
                ins.then_inc(s_cf, 1)
                for t in range(b * NQ, (b + 1) * NQ):
                    ins = dve.scalar_tensor_tensor(out=qn[:, t, 0:QL], in0=pr[:, t, cQ:cQ + QL], scalar=ms[:, t, 0:1],
                                                   in1=qwb[:, :], op0=ALU.mult, op1=ALU.mult)
                ins.then_inc(s_qn, 1)

            variance(0)
            variance(1)
            normalise(0)
            variance(2)
            normalise(1)
            low_x(0)
            for t in range(NT):
                if t + 3 < NT:
                    variance(t + 3)
                if t + 2 < NT:
                    normalise(t + 2)
                if t + 1 < NT:
                    low_x(t + 1)
                squares(t)
                if t == 0:
                    dve.wait_ge(s_const, 16 * CONSTS)
                    dve.tensor_scalar(kvs[:, :], kvcol[:, :], 1.0 / PS, None, ALU.mult)
                if t == NT - 3:
                    latents(0)

            def low_kq(t):
                dve.wait_ge(s_qkh, t + 1)
                src = bank[4 + t % 2]
                c = slice(t * P, (t + 1) * P)
                dve.tensor_tensor(kTl[:, c], src[:, 0:P], kTh[:, c].bitcast(f32), ALU.subtract)
                dve.tensor_tensor(R2[:, c], src[:, P:2 * P], R1[:, c].bitcast(f32), ALU.subtract)
                dve.tensor_tensor(R3[KL:P, c], src[KL:P, 2 * P:3 * P], R3[KL:P, c].bitcast(f32), ALU.subtract)\
                   .then_inc(s_qkl, 1)

            def drain(it, item):
                kind, i = item
                r = RING[item]
                src = rBank[r % 2]
                if kind == "A":
                    dve.wait_ge(s_hi, W(it, HI[item] + 1, HPI))
                    dst = QWh[i % 2][:, :, :, 0:KL]
                    dve.tensor_tensor(QWl[i % 2][:, :, :, 0:KL], src[:, 0:4 * KL].rearrange("p (c h k) -> p c h k", c=2, h=2),
                                      dst.bitcast(f32), ALU.subtract).then_inc(s_drained, 1)
                if kind == "M":
                    dve.wait_ge(s_hi, W(it, HI[item] + 1, HPI))
                    dve.scalar_tensor_tensor(out=Ml[:, i % GP, :], in0=src[:, :], scalar=kvs[:, 0:1],
                                             in1=Mh[:, i % GP, :].bitcast(f32), op0=ALU.mult, op1=ALU.subtract)\
                       .then_inc(s_drained, 1)
                if kind == "OT":
                    dve.wait_ge(s_hi, W(it, HI[item] + 1, HPI))
                    j, c = (i // B) % GP, slice((i % B) * S, (i % B + 1) * S)
                    dve.tensor_tensor(OTl[:, j, c], src[:, :], OTh[:, j, c].bitcast(f32), ALU.subtract)\
                       .then_inc(s_drained, 1)
                if kind == "q":
                    dve.wait_ge(s_full, W(it, r + 1, RPI))
                    if i >= 2:
                        dve.wait_ge(s_ql, W(it, i - 1, UPI))
                    dve.tensor_tensor(q32[i % 2][:, :], src[:, :], CQ[:, :], ALU.mult)
                    dve.stream_shuffle(qs[i % 2][KL:P, :], src[KL:P, :], SWAP).then_inc(s_drained, 1)
                if kind == "HT":
                    dve.wait_ge(s_full, r + 1)
                    dve.tensor_copy(hwT[:, 4 * i:4 * i + 4, :], src[:, :].rearrange("p (t c) -> p t c", t=4))\
                       .then_inc(s_drained, 1)
                if kind == "ffn":
                    dve.wait_ge(s_full, r + 1)
                    dve.tensor_tensor(gate[:, i, :], src[:, :], bbb[:, :], ALU.add).then_inc(s_drained, 1)
                if kind == "out":
                    t = i % NT
                    dve.wait_ge(s_full, W(it, r + 1, RPI))
                    if i == 0 or not isinstance(it, int):
                        dve.wait_ge(s_acc0, 1)
                    ins = dve.tensor_tensor(acc[:, t, :], acc[:, t, :], src[:, :], ALU.add)
                    ins.then_inc(s_drained, 1)
                    if i >= NT * (NI - 1):
                        dve.wait_ge(s_drained, r + 1)
                        dve.wait_ge(s_g, t + 1)
                        dve.tensor_tensor(acc[:, t, :], acc[:, t, :], gate[:, t, :], ALU.mult).then_inc(s_fm, 1)

            for t in range(NQ):
                low_kq(t)
            drain(0, START[0])
            latents(1)
            for item in START[1:]:
                drain(0, item)
            for t in range(NQ, NT):
                low_kq(t)

            for t in range(NT):
                ins = dve.max(top[:, t, :], pr[:, t, cL:cL + NE])
            link(ins)
            dve.tensor_tensor(gap[:, :], top[:, :, 1], top[:, :, 0], ALU.subtract).then_inc(s_ed, 1)
            for t in range(NT):
                ins = dve.max_index(topi[:, t, :], top[:, t, :], pr[:, t, cL:cL + NE])
            link(ins)
            link(dve.tensor_copy(idx[:, :, :], topi[:, :, 0:2]))
            row = iota[:, :].unsqueeze(1).to_broadcast([P, NT, NE])
            for j in range(2):
                dve.tensor_tensor(oh[:, j, :, :], row, idx[:, :, j:j + 1].to_broadcast([P, NT, NE]), ALU.is_equal)
            dve.wait_ge(s_ex, 1)
            link(dve.tensor_scalar(p12[:, 1, :], eg[:, :], 1.0, 1.0 / LORA_SCALE, ALU.add, ALU.mult))
            link(dve.reciprocal(p12[:, 0, :], p12[:, 1, :]))
            link(dve.tensor_tensor(p12[:, 1, :], eg[:, :], p12[:, 0, :], ALU.mult))
            for j in range(2):
                ins = dve.tensor_tensor(oh[:, j, :, :], oh[:, j, :, :],
                                        p12[:, j, :].unsqueeze(2).to_broadcast([P, NT, NE]), ALU.mult)
            link(ins)
            dve.tensor_tensor(oh[:, 0, :, :], oh[:, 0, :, :], oh[:, 1, :, :], ALU.add).then_inc(s_wt, 1)

            def row_max(it, n):
                w = (n % NQ + 1) * P
                dve.wait_ge(s_S, W(it, n + 1, SPI))
                dve.tensor_reduce(nmax[:, n % 8:n % 8 + 1], sBank[n % 2][:, 0:w], AX.X, ALU.max, negate=True)\
                   .then_inc(s_max, 1)

            def low_probs(it, n):
                w = (n % NQ + 1) * P
                dve.wait_ge(s_ph, W(it, n + 1, SPI))
                dve.scalar_tensor_tensor(out=Pl[n % 4][:, 0:w], in0=tBank[n % 2][:, 0:w], scalar=PS,
                                         in1=Ph[n % 4][:, 0:w], op0=ALU.mult, op1=ALU.subtract).then_inc(s_pl, 1)

            def normalise_block(it, ob):
                dve.wait_ge(s_PV, W(it, NQ * HP * (ob + 1), SPI))
                dve.reciprocal(rinv[:, ob % 2, :], sums[:, ob % 4, :]).then_inc(s_ri, 1)
                dve.wait_ge(s_ri, W(it, ob + 1, OPI))
                dve.tensor_tensor(osb[ob % 2][:, :, :].rearrange("p q (h c) -> p (q h) c", h=HP),
                                  oBank[ob % 2][:, :].rearrange("p (m c) -> p m c", c=KL),
                                  rinv[:, ob % 2, :].unsqueeze(2).to_broadcast([P, NQ * HP, KL]), ALU.mult)\
                   .then_inc(s_o, 1)

            def step(it, k, s):
                n = SPI * k + s
                if n + 2 < NN:
                    row_max(it, n + 2)
                low_probs(it, n)
                if s % 8 == 2 and n > 8:
                    normalise_block(it, OPI * k + s // 8 - 1)
                for item in fillers(k, s):
                    drain(it, item)

            row_max(0, 0)
            row_max(0, 1)
            for s in range(SPI):
                step(0, 0, s)
            with dve.Fori(1, NI - 1) as i:
                for s in range(SPI):
                    step(i, 1, s)
            for s in range(SPI):
                step(NI - 1, NI - 1, s)
            normalise_block(0, NO - 1)
            for item in DRAIN:
                drain(0, item)


HI = {}
for _item in RING:
    if _item[0] in ("A", "M", "OT"):
        HI[_item] = len(HI)
HPI = 2 * GP + OPI

_OUTS = [((B, S, D), "float32")]


def _tables():
    import numpy as np
    freqs = (1.0 / 10000.0 ** (np.arange(0, ROPE, 2, dtype=np.float32) / np.float32(ROPE))).astype(np.float32)
    ang = np.outer(np.arange(S, dtype=np.float32), freqs).astype(np.float32)
    cos, sin = np.cos(ang).astype(np.float32), np.sin(ang).astype(np.float32)
    c2 = np.repeat(cos, 2, axis=1)
    s2 = np.stack([-sin, sin], axis=-1).reshape(S, ROPE)
    scale = np.float32(float(NOPE + ROPE) ** -0.5)
    cosq = np.concatenate([np.ones((KL, S), np.float32), c2.T], axis=0)
    sinq = np.concatenate([np.zeros((KL, S), np.float32), s2.T], axis=0)
    cosk = (c2 * scale).reshape(NQ, P, ROPE).transpose(1, 0, 2)
    sink = (s2 * scale).reshape(NQ, P, ROPE).transpose(1, 0, 2)
    mask = np.triu(np.full((P, P), MASKED, np.float32), 1)
    return cosq, sinq, cosk, sink, np.eye(P, dtype=np.float32), mask, np.tile(np.arange(NE, dtype=np.float32), (P, 1))


def kernel(**inputs):
    import numpy as np
    import ml_dtypes
    import concourse.bacc as _bacc
    from concourse.bass_utils import run_bass_kernel_spmd as _run

    a = {k.replace("L0_attn_", "").replace("L0_ffn_", ""): np.asarray(v) for k, v in inputs.items()}

    def by_rows(w):
        return w.reshape(KD, P, -1).transpose(1, 0, 2)

    w1 = by_rows(np.concatenate([a["wq_a"].T, a["wkv_a"].T, a["lora_A"].reshape(NE * R, D).T, a["W_router"].T], axis=1))
    wb = by_rows(a["W_base"].T)
    lbt = a["lora_B"].transpose(0, 2, 1).reshape(NE * R, D)
    wqb = a["wq_b"].reshape(NP, HP, NOPE + ROPE, QL)
    nope = wqb[:, :, :NOPE, :].transpose(0, 2, 1, 3)
    nope = np.concatenate([nope, nope[..., P:QL]], axis=-1).reshape(NP, P, HP * 256)
    rope = wqb[:, :, NOPE:, :].transpose(0, 3, 1, 2)
    rope = np.stack([rope[:, 0:P], np.concatenate([rope[:, P:QL], rope[:, P:QL]], axis=1)], axis=2)
    rope = rope.reshape(NP, P, 2 * HP * ROPE)
    wkv = a["wkv_b"].reshape(NP, HP, 2, P, KL).transpose(0, 3, 2, 1, 4).reshape(NP, P, 2 * HP * KL)
    wo = a["wo"].T.reshape(NP, HP, VD, D).transpose(0, 2, 1, 3).reshape(NP, P, HP * D)
    wp = np.concatenate([nope, rope, wkv, wo], axis=-1)
    cosq, sinq, cosk, sink, ident, mask, iota = _tables()
    arrays_in = [a["x"], w1, wb, lbt, wp, a["q_norm_w"], a["kv_norm_w"], a["b_base"], cosq, sinq, cosk, sink,
                 ident, mask.astype(ml_dtypes.bfloat16), ident.astype(ml_dtypes.bfloat16), iota]
    names = ["x", "w1", "wb", "lbt", "wp", "qw", "kvw", "bb", "cosq", "sinq", "cosk", "sink", "ident", "mask",
             "identb", "iota"]
    nc = _bacc.Bacc("TRN2", target_bir_lowering=False, num_devices=1)
    arrays, args = {}, []
    for name, v in zip(names, arrays_in):
        v = np.ascontiguousarray(v)
        arrays[f"in_{name}"] = v
        args.append(nc.dram_tensor(f"in_{name}", v.shape, mybir.dt.from_np(v.dtype), kind="ExternalInput").ap())
    args.append(nc.dram_tensor("out_0", _OUTS[0][0], f32, kind="ExternalOutput").ap())
    attention_kernel(nc, *args)
    r = _run(nc, [arrays], core_ids=[0])
    return r.results[0]["out_0"]
```

```python
import concourse.bass as bass
from concourse import mybir
from contextlib import ExitStack

f32 = mybir.dt.float32
f32r = mybir.dt.float32r
f16 = mybir.dt.float16
bf16 = mybir.dt.bfloat16
u32 = mybir.dt.uint32
ALU = mybir.AluOpType
ACT = mybir.ActivationFunctionType
AX = mybir.AxisListType

P = 128
B, S, D = 2, 512, 512
NT = B * S // P
KD = D // P
NH, NOPE, ROPE, VD = 32, 128, 64, 128
QL, KL = 192, 64
NE, R = 8, 16
EPS_LN, EPS_RMS = 1e-5, 1e-6
LORA_SCALE = 32.0 / 16.0
NQ = S // P
GT = 2
HP = 2
NP = NH // HP
GP = 2
NI = NP // GP
UPI = GP * B * HP
NU = NI * UPI
SPI = UPI * NQ
NN = NU * NQ
OPI = GP * B
NO = NI * OPI
C1 = QL + KL + ROPE + NE * R + NE
cQ, cC, cK, cH, cL = 0, QL, QL + KL, QL + KL + ROPE, QL + KL + ROPE + NE * R
PS = 1024.0
MASKED = -1e37
GV = 2
NB = 4
CONSTS = 9

wQ = 0
wR = wQ + HP * 256
wK = wR + 2 * HP * ROPE
WAF = wK + HP * KL
wV = 0
wO = wV + HP * KL
WMF = wO + HP * D


def fillers(it, s):
    pair, uu, qt = it * GP + s // 16, (s % 16) // 4, s % 4
    out = []
    if qt == 2 and UPI * it + s // 4 + 3 < NU:
        out.append(("q", UPI * it + s // 4 + 3))
    if uu == 0 and qt == 3 and pair + 1 < NP:
        out.append(("A", pair + 1))
    if s % 8 == 5 and OPI * it + s // 8 >= 1:
        out.append(("OT", OPI * it + s // 8 - 1))
    if s in (4, 5) and it == 0:
        out.append(("HT", s - 4))
    if s in OUT_STEPS:
        out.append(("out", NT * (it - 1) + OUT_STEPS.index(s)) if it else ("ffn", OUT_STEPS.index(s)))
    if s in M_STEPS:
        out.append(("M", GP * it + M_STEPS.index(s)))
    return out


OUT_STEPS = [7, 8, 11, 12, 15, 16, 17, 20]
M_STEPS = [24, 27]
SWAP = [i ^ 1 for i in range(32)]
START = [("A", 0), ("q", 0), ("q", 1), ("q", 2)]
DRAIN = [("out", NT * (NI - 1) + t) for t in range(NT)]
DRAIN.insert(2, ("OT", NO - 1))
RING = {}
for _item in START + [i for it in range(NI) for s in range(SPI) for i in fillers(it, s)] + DRAIN:
    RING[_item] = len(RING)
ORDER = list(RING)
DR = {_item: _n + 1 for _n, _item in enumerate(i for i in ORDER if i[0] != "q")}
RPI = sum(len(fillers(1, s)) for s in range(SPI))
DPI = RPI - UPI


def W(it, value, rate):
    return value if isinstance(it, int) else it * rate + (value - rate)


def attention_kernel(nc, x, w1, wb, lbt, wp, qw, kvw, bb, cosq, sinq, cosk, sink, identd, maskd, identbd,
                     iotad, out):
    ctx = ExitStack()
    with ctx:
        def sb(name, shape, dt=f32):
            return ctx.enter_context(nc.sbuf_tensor(name, shape, dt))

        def sem(name):
            return ctx.enter_context(nc.semaphore(name))

        bank = [ctx.enter_context(nc.psum_tensor(f"bank{i}", [P, 512], f32)) for i in range(8)]
        sBank, tBank, oBank, rBank = bank[0:2], bank[2:4], bank[4:6], bank[6:8]

        ident = sb("ident", [P, P])
        identb = sb("identb", [P, P], bf16)
        mask = sb("mask", [P, P], bf16)
        CQ = sb("CQ", [P, S])
        SQ = sb("SQ", [P, S])
        CK = sb("CK", [P, NQ, ROPE])
        SK = sb("SK", [P, NQ, ROPE])
        qwb = sb("qwb", [P, QL])
        kvwb = sb("kvwb", [P, KL])
        kvcol = sb("kvcol", [P, 1])
        kvs = sb("kvs", [P, 1])
        bbb = sb("bbb", [P, D])
        iota = sb("iota", [P, NE])
        lbT = sb("lbT", [P, D])

        kTh, kTl = sb("kTh", [P, B * S], f32r), sb("kTl", [P, B * S], f32r)
        ch, cl = sb("ch", [P, NT, KL], f16), sb("cl", [P, NT, KL], f16)
        R1, R2, R3 = (sb(f"R{i}", [P, B * S], f32r) for i in (1, 2, 3))
        gate = sb("gate", [P, NT, D])
        Wbuf = sb("Wbuf", [P, 2 * (WAF + WMF)])
        WA = [Wbuf[:, i * WAF:(i + 1) * WAF] for i in range(2)]
        WM = [Wbuf[:, 2 * WAF + i * WMF:2 * WAF + (i + 1) * WMF] for i in range(2)]
        with ExitStack() as early:
            wbh, wbl = (early.enter_context(nc.sbuf_tensor(n, [P, KD, D], f32r)) for n in ("wbh", "wbl"))
        acc = sb("acc", [P, NT, D])
        xTh, xTl = sb("xTh", [P, KD, B * S], f32r), sb("xTl", [P, KD, B * S], f32r)
        hwT = sb("hwT", [P, NT, P])
        w1raw = Wbuf[:, 0:KD * C1].rearrange("p (k c) -> p k c", k=KD)
        wbraw = Wbuf[:, KD * D:2 * KD * D].rearrange("p (k c) -> p k c", k=KD)
        QWh = [sb(f"QWh{i}", [P, 2, HP, P], f32r) for i in range(2)]
        QWl = [sb(f"QWl{i}", [P, 2, HP, P], f32r) for i in range(2)]
        q32 = [sb(f"q32_{i}", [P, S]) for i in range(2)]
        qs = [sb(f"qs{i}", [P, S]) for i in range(2)]
        Ph = [sb(f"probsTh{i}", [P, S], f16) for i in range(4)]
        Pl = [sb(f"probsTl{i}", [P, S], f16) for i in range(4)]
        nmax = sb("nmax", [P, 8])
        sums = sb("sums", [P, 4, NQ * HP])
        rinv = sb("rinv", [P, 2, NQ * HP])

        s_x = [sem(f"x{t}") for t in range(NT)]
        s_const, s_kconst, s_wbd = sem("constants_loaded"), sem("latent_constants_loaded"), sem("wb_loaded")
        s_w1d = [sem(f"w1_half{i}_loaded") for i in range(2)]
        s_wa = [sem(f"query_weights{i}_loaded") for i in range(2)]
        s_wm = [sem(f"merge_weights{i}_loaded") for i in range(2)]
        s_w1h, s_w1l, s_wbh, s_wbl = sem("w1_high"), sem("w1_low"), sem("wb_high"), sem("wb_low")
        s_dv, s_sq = sem("vector_chain"), sem("sqrt_done")
        s_rms = sem("rms_done")
        s_varq, s_eps = sem("variance_ready"), sem("eps_set")
        s_xn, s_xt, s_xh, s_xl = sem("xn_ready"), sem("xT_psum"), sem("xT_high"), sem("xT_low")
        s_pr, s_prc = sem("proj_psum"), sem("proj_copied")
        s_id, s_cf, s_qn, s_qd, s_kc, s_ch = (sem("identity_loaded"), sem("latents_normed"), sem("qn_ready"),
                                              sem("qn_doubled"), sem("kc_ready"), sem("latents_high"))
        s_ms = sem("mean_squares_ready")
        s_qk, s_qkh, s_qkl = sem("kcqn_psum"), sem("kcqn_high"), sem("kcqn_low")
        s_pool = sem("gpsimd_chain")
        s_ed, s_ex = sem("router_gap_ready"), sem("router_exp")
        s_hw, s_wt = sem("lora_hidden_ready"), sem("expert_weights_ready")
        s_sig, s_g = sem("sigmoid_ready"), sem("gate_ready")
        s_full, s_drained = sem("filler_psum"), sem("filler_drained")
        s_hi = sem("filler_high")
        s_wrh, s_wr = sem("rope_weights_high"), sem("rope_weights_split")
        s_sw = [sem(f"q_swapped{i}") for i in range(2)]
        s_qc, s_qv, s_qa, s_qh, s_ql = sem("q_copied"), sem("q_sin"), sem("q_roped"), sem("q_high"), sem("q_low")
        s_S, s_max, s_exp = sem("scores"), sem("row_max"), sem("row_exp")
        s_T, s_ph, s_pl = sem("probsT"), sem("probsT_high"), sem("probsT_low")
        s_PV, s_ri, s_o = sem("latent_out"), sem("row_sums_inverted"), sem("latent_out_normed")
        s_acc0 = sem("acc_zeroed")
        s_fm, s_fx, s_xr, s_out = sem("gated"), sem("residual_added"), sem("x_reloaded"), sem("stored")

        s_last = sem("last_tile_done")
        s_base, s_based = sem("base_psum"), sem("base_drained")

        def unit_of(n):
            return n // NQ

        start_ctx = ExitStack()

        def st(name, shape, dt=f32):
            return start_ctx.enter_context(nc.sbuf_tensor(name, shape, dt))

        w1h, w1l = st("w1h", [P, KD, C1], f32r), st("w1l", [P, KD, C1], f32r)
        xin = [st(f"xin{i}", [P, D]) for i in range(4)]
        xn = [st(f"xn{i}", [P, D]) for i in range(2)]
        pr = st("pr", [P, NT, C1])
        qn = st("qn", [P, NT, 256])
        kc = st("kc", [P, NT, KL + ROPE])
        eps = st("eps", [P, 1])
        early_root = st("early_root", [P, 1])
        stats = st("stats", [P, NT, 6])
        mv = st("mv", [P, NT, 2])
        rstd = st("rstd", [P, NT])
        ms = st("ms", [P, NT, 2])
        cf = st("cf", [P, NT, KL])
        t2 = st("t2", [P, NT, ROPE])
        top = st("top", [P, NT, 8])
        topi = st("topi", [P, NT, 8], u32)
        idx = st("idx", [P, NT, 2])
        gap = st("gap", [P, NT])
        eg = st("eg", [P, NT])
        p12 = st("p12", [P, 2, NT])
        oh = st("oh", [P, 2, NT, NE])
        kvw_s = st("kvw_s", [P, KL])
        hw = st("hw", [P, NT, NE * R])
        start_ctx.close()
        qh = [sb(f"qh{i}", [P, S], f32r) for i in range(4)]
        ql = [sb(f"ql{i}", [P, S], f32r) for i in range(4)]
        sig = [t[:, :] for t in q32 + qs + [CQ, SQ, bbb, lbT]]
        Pr = [sb(f"probs{i}", [P, S]) for i in range(4)]
        osb = [sb(f"osb{i}", [P, NQ, P]) for i in range(2)]
        OTh, OTl = sb("OTh", [P, GP, B * S], f32r), sb("OTl", [P, GP, B * S], f32r)
        Mh, Ml = sb("Mh", [P, GP, D], f32r), sb("Ml", [P, GP, D], f32r)

        block = ctx.enter_context(nc.Block())
        x_t = x.rearrange("b (q p) d -> p (b q) d", p=P)
        out_t = out.rearrange("b (q p) d -> p (b q) d", p=P)
        xres = [Wbuf[:, t * D:(t + 1) * D] for t in range(NT)]

        @block.sync
        def _(sp):
            def load_x(t):
                if t >= 4:
                    sp.wait_ge(s_xn, t - 3)
                sp.dma_start(xin[t % 4][:, :], x_t[:, t, :]).then_inc(s_x[t], 16)

            for t in range(4):
                load_x(t)
            sp.dma_start(CK[:, :, :], cosk).then_inc(s_kconst, 16)
            sp.dma_start(SK[:, :, :], sink).then_inc(s_kconst, 16)
            sp.dma_start(qwb[:, :], qw.partition_broadcast(P)).then_inc(s_kconst, 16)
            sp.dma_start(kvwb[:, :], kvw.partition_broadcast(P)).then_inc(s_kconst, 16)
            sp.dma_start(wbraw, wb).then_inc(s_wbd, 16)
            for t in range(4, NT):
                load_x(t)

            def load(it, p, pair, which):
                if which == 0:
                    sp.dma_start(WA[p % 2], wp[pair, :, 0:WAF]).then_inc(s_wa[p % 2], 16)
                else:
                    sp.dma_start(WM[p % 2], wp[pair, :, WAF:WAF + WMF]).then_inc(s_wm[p % 2], 16)

            sp.wait_ge(s_w1l, 2)
            load(0, 0, 0, 0)
            for dst, src in ((CQ, cosq), (SQ, sinq), (identb, identbd), (mask, maskd), (iota, iotad), (lbT, lbt)):
                sp.dma_start(dst[:], src).then_inc(s_const, 16)
            sp.dma_start(bbb[:, :], bb.partition_broadcast(P)).then_inc(s_const, 16)
            for h in range(HP):
                sp.dma_start(kvcol[h * KL:(h + 1) * KL, :], kvw.rearrange("(c a) -> c a", a=1)).then_inc(s_const, 16)
            load(0, 1, 1, 0)
            sp.wait_ge(s_wbl, KD)
            load(0, 0, 0, 1)
            load(0, 1, 1, 1)
            sp.wait_ge(s_drained, DR["A", 0])
            sp.wait_ge(s_wr, 1)
            load(0, 2, 2, 0)

            def swap(it, u):
                i = u % 2
                sp.wait_ge(s_qc, W(it, u + 1, UPI))
                sp.dma_start(qs[i][KL:P:2, :], q32[i][KL + 1:P:2, :]).then_inc(s_sw[i], 16)
                sp.dma_start(qs[i][KL + 1:P:2, :], q32[i][KL:P:2, :]).then_inc(s_sw[i], 16)

            def step(it, k, s):
                for kind, p in fillers(k, s):
                    if kind == "q":
                        swap(it, p)
                for kind, p in fillers(k, s - 3) if s >= 3 else ():
                    if kind in ("A", "M") and p + 2 < NP:
                        sp.wait_ge(s_drained, W(it, DR[kind, p], DPI))
                        if kind == "A":
                            sp.wait_ge(s_wr, W(it, p + 1, GP))
                        nxt = p + 2 if isinstance(it, int) else sp.snap(it * GP + (p + 2 - GP * k))
                        load(it, p, nxt, 0 if kind == "A" else 1)

            for s in range(SPI):
                step(0, 0, s)
            with sp.Fori(1, NI - 2) as i:
                for s in range(SPI):
                    step(i, 1, s)
            for k in (NI - 2, NI - 1):
                for s in range(SPI):
                    step(k, k, s)
            sp.wait_ge(s_drained, DR["M", NP - 1])
            sp.dma_start(Wbuf[:, :].rearrange("p (t d) -> p t d", t=NT), x_t).then_inc(s_xr, 16)
            for t in range(NT):
                if t < NT - 1:
                    sp.wait_ge(s_fx, t + 1)
                else:
                    sp.wait_ge(s_last, 1)
                sp.dma_start(out_t[:, t, :], acc[:, t, :]).then_inc(s_out, 16)
            sp.wait_ge(s_out, 16 * NT)

        @block.tensor
        def _(pe):
            pe.wait_ge(s_id, 16)
            three = ((0, 0), (0, 1), (1, 0))

            def x_transposes(t):
                pe.wait_ge(s_xn, t + 1)
                if t >= 2:
                    pe.wait_ge(s_xl, t - 1)
                for k in range(KD):
                    mm = pe.transpose(bank[t % 2][:, k * P:(k + 1) * P], xn[t % 2][:, k * P:(k + 1) * P], ident[:, :])
                mm.then_inc(s_xt, 1)

            def project(t):
                pe.wait_ge(s_xl, t + 1)
                if t >= 2:
                    pe.wait_ge(s_prc, t - 1)
                n, tok = 0, slice(t * P, (t + 1) * P)
                for k in range(KD):
                    if t == 0 and k % 2 == 0:
                        pe.wait_ge(s_w1l, k // 2 + 1)
                    for a, b in three:
                        mm = pe.matmul(bank[2 + t % 2][:, 0:C1], (xTh, xTl)[a][:, k, tok],
                                       (w1h, w1l)[b][:, k, :], start=(n == 0), stop=(n == 3 * KD - 1))
                        n += 1
                mm.then_inc(s_pr, 1)

            def key_query_transposes(t):
                if t % GT == 0:
                    g = t // GT
                    pe.wait_ge(s_kc, g + 1)
                    pe.wait_ge(s_qn, g + 1)
                    pe.wait_ge(s_qd, g + 1)
                if t >= 2:
                    pe.wait_ge(s_qkl, t - 1)
                for j, src in enumerate((kc[:, t, :], qn[:, t, 0:P], qn[:, t, P:2 * P])):
                    mm = pe.transpose(bank[4 + t % 2][:, j * P:(j + 1) * P], src, ident[:, :])
                mm.then_inc(s_qk, 1)

            def ring_slot(it, item):
                r = RING[item]
                if r >= 2:
                    kind, i = ORDER[r - 2]
                    if kind == "q":
                        pe.wait_ge(s_qc, W(it, i + 1, UPI))
                    else:
                        pe.wait_ge(s_drained, W(it, DR[kind, i], DPI))
                return rBank[r % 2]

            def absorb(it, p):
                dst = ring_slot(it, ("A", p))
                pe.wait_ge(s_wa[p % 2], W(it, 16 * (p // 2 + 1), 16 * GP // 2))
                w = WA[p % 2]
                for c in range(2):
                    for h in range(HP):
                        o = (c * HP + h) * KL
                        mm = pe.matmul(dst[:, o:o + KL], w[:, wQ + h * 256 + c * P:wQ + h * 256 + (c + 1) * P],
                                       w[:, wK + h * KL:wK + (h + 1) * KL], start=True, stop=True)
                mm.then_inc(s_full, 1)

            def query(it, u):
                p, b, h = u // 4, (u // 2) % 2, u % 2
                dst = ring_slot(it, ("q", u))
                if u % 4 == 0:
                    pe.wait_ge(s_drained, W(it, DR["A", p], DPI))
                    pe.wait_ge(s_wr, W(it, p + 1, GP))
                h_, l_ = QWh[p % 2], QWl[p % 2]
                cols = slice(b * S, (b + 1) * S)
                work = ((h_, 0, R1), (h_, 0, R2), (l_, 0, R1), (h_, 1, R3), (l_, 1, R3))
                for n, (w, c, r) in enumerate(work):
                    mm = pe.matmul(dst[:, :], w[:, c, h, :], r[:, cols], start=(n == 0), stop=(n == 4))
                mm.then_inc(s_full, 1)

            def merge(it, p):
                dst = ring_slot(it, ("M", p))
                pe.wait_ge(s_wm[p % 2], W(it, 16 * (p // 2 + 1), 16 * GP // 2))
                w = WM[p % 2]
                for h in range(HP):
                    mm = pe.matmul(dst[h * KL:(h + 1) * KL, :], w[:, wV + h * KL:wV + (h + 1) * KL],
                                   w[:, wO + h * D:wO + (h + 1) * D], start=True, stop=True)
                mm.then_inc(s_full, 1)

            def out_transposes(it, ob):
                dst = ring_slot(it, ("OT", ob))
                pe.wait_ge(s_o, W(it, ob + 1, OPI))
                for q in range(NQ):
                    mm = pe.transpose(dst[:, q * P:(q + 1) * P], osb[ob % 2][:, q, :], ident[:, :])
                mm.then_inc(s_full, 1)

            def out_project(it, ot):
                g, t = ot // NT, ot % NT
                dst = ring_slot(it, ("out", ot))
                if t % NQ == 0:
                    pe.wait_ge(s_drained, W(it, DR["OT", OPI * (g + 1) - 2 + t // NQ], DPI))
                n = 0
                for j in range(GP):
                    for a, b in three:
                        mm = pe.matmul(dst[:, :], (OTh, OTl)[a][:, j, t * P:(t + 1) * P], (Mh, Ml)[b][:, j, :],
                                       start=(n == 0), stop=(n == 3 * GP - 1))
                        n += 1
                mm.then_inc(s_full, 1)

            def lora_transposes(it, g):
                dst = ring_slot(it, ("HT", g))
                pe.wait_ge(s_hw, 1)
                for j in range(4):
                    mm = pe.transpose(dst[:, j * P:(j + 1) * P], hw[:, 4 * g + j, :], ident[:, :])
                mm.then_inc(s_full, 1)

            def base_products(dst, t, last):
                n, tok = 0, slice(t * P, (t + 1) * P)
                for k in range(KD):
                    for a, b in three:
                        mm = pe.matmul(dst[:, :], (xTh, xTl)[a][:, k, tok], (wbh, wbl)[b][:, k, :],
                                       start=(n == 0), stop=(last and n == 3 * KD - 1))
                        n += 1
                return mm

            def base(t):
                if t == 0:
                    pe.wait_ge(s_wbl, KD)
                    pe.wait_ge(s_prc, NT)
                if t >= 2:
                    pe.wait_ge(s_based, t - 1)
                base_products(tBank[t % 2], t, True).then_inc(s_base, 1)

            def linear(it, t):
                dst = ring_slot(it, ("ffn", t))
                if t == 0:
                    pe.wait_ge(s_drained, DR["HT", 1])
                if t >= NB:
                    base_products(dst, t, False)
                pe.matmul(dst[:, :], hwT[:, t, :], lbT[:, :], start=(t < NB), stop=True).then_inc(s_full, 1)

            fill = {"HT": lora_transposes, "ffn": linear, "A": absorb, "q": query, "M": merge,
                    "OT": out_transposes, "out": out_project}

            def scores(it, n):
                u, qt = unit_of(n), n % NQ
                b = (u // 2) % 2
                if qt == 0:
                    pe.wait_ge(s_ql, W(it, u + 1, UPI))
                w = (qt + 1) * P
                dst = sBank[n % 2]
                for m, (a, k) in enumerate(((qh, kTh), (qh, kTl), (ql, kTh))):
                    pe.matmul(dst[:, 0:w], a[u % 4][:, qt * P:(qt + 1) * P], k[:, b * S:b * S + w],
                              start=(m == 0), stop=False)
                pe.matmul(dst[:, w - P:w], identb[:, :], mask[:, :], start=False, stop=True).then_inc(s_S, 1)

            def transposes(it, n):
                pe.wait_ge(s_exp, W(it, n + 1, SPI))
                if n >= 2:
                    pe.wait_ge(s_pl, W(it, n - 1, SPI))
                for k in range(n % NQ + 1):
                    mm = pe.transpose(tBank[n % 2][:, k * P:(k + 1) * P], Pr[n % 4][:, k * P:(k + 1) * P], ident[:, :])
                mm.then_inc(s_T, 1)

            def times_latents(it, n):
                u, qt = unit_of(n), n % NQ
                b, h, ob = (u // 2) % 2, u % 2, u // 2
                pe.wait_ge(s_pl, W(it, n + 1, SPI))
                if h == 0 and qt == 0 and ob >= 2:
                    pe.wait_ge(s_o, W(it, ob - 1, OPI))
                dst = oBank[ob % 2][:, (qt * HP + h) * KL:(qt * HP + h + 1) * KL]
                m, last = 0, 3 * (qt + 1) - 1
                for k in range(qt + 1):
                    for a, c in ((Ph, ch), (Ph, cl), (Pl, ch)):
                        mm = pe.matmul(dst, a[n % 4][:, k * P:(k + 1) * P], c[:, b * NQ + k, :],
                                       start=(m == 0), stop=(m == last))
                        m += 1
                mm.then_inc(s_PV, 1)

            x_transposes(0)
            for t in range(NT):
                if t + 1 < NT:
                    x_transposes(t + 1)
                project(t)
                if t == 3:
                    key_query_transposes(0)
                    key_query_transposes(1)
                if t == 4:
                    absorb(0, 0)
                if t == 5:
                    key_query_transposes(2)
                    key_query_transposes(3)
                if t == 6:
                    pe.wait_ge(s_qkl, NQ)
                    query(0, 0)
            query(0, 1)
            base(0)
            key_query_transposes(4)
            key_query_transposes(5)
            base(1)
            key_query_transposes(6)
            key_query_transposes(7)
            base(2)

            def step(it, k, s):
                n = SPI * k + s
                transposes(it, n)
                if n + 2 < NN:
                    scores(it, n + 2)
                for kind, i in fillers(k, s):
                    fill[kind](it, i)
                if n >= 2:
                    times_latents(it, n - 2)

            pe.wait_ge(s_xl, NT)
            pe.wait_ge(s_prc, NT)
            pe.wait_ge(s_const, 16 * CONSTS)
            pe.wait_ge(s_qkl, NT)
            scores(0, 0)
            scores(0, 1)
            query(0, 2)
            base(3)
            pe.wait_ge(s_based, NB)
            for s in range(SPI):
                step(0, 0, s)
            with pe.Fori(1, NI - 1) as i:
                for s in range(SPI):
                    step(i, 1, s)
            for s in range(SPI):
                step(NI - 1, NI - 1, s)
            for n in (NN - 2, NN - 1):
                kind, i = DRAIN[n - NN + 2]
                fill[kind](0, i)
                times_latents(0, n)
            for kind, i in DRAIN[2:]:
                fill[kind](0, i)

        @block.scalar
        def _(act):
            act.dma_start(ident[:, :], identd).then_inc(s_id, 16)
            for i in range(2):
                act.dma_start(w1raw[:, 2 * i:2 * i + 2, :], w1[:, 2 * i:2 * i + 2, :]).then_inc(s_w1d[i], 16)

            def high_x(t):
                act.wait_ge(s_xt, t + 1)
                act.activation(xTh[:, :, t * P:(t + 1) * P], bank[t % 2][:, :].rearrange("p (k t) -> p k t", k=KD),
                               ACT.Copy).then_inc(s_xh, 1)

            def copy_projection(t):
                act.wait_ge(s_pr, t + 1)
                act.activation(pr[:, t, :], bank[2 + t % 2][:, 0:C1], ACT.Copy).then_inc(s_prc, 1)

            def root(t):
                act.wait_ge(s_varq, t + 1)
                act.activation(rstd[:, t:t + 1], mv[:, t, 1:2], ACT.Sqrt, bias=eps[:, 0:1]).then_inc(s_sq, 1)

            def high_w1(i):
                act.wait_ge(s_w1d[i], 16)
                act.activation(w1h[:, 2 * i:2 * i + 2, :], w1raw[:, 2 * i:2 * i + 2, :], ACT.Copy).then_inc(s_w1h, 1)

            def rms_roots(g):
                act.wait_ge(s_ms, g + 1)
                act.activation(ms[:, g * GT:(g + 1) * GT, :], ms[:, g * GT:(g + 1) * GT, :], ACT.Sqrt).then_inc(s_rms, 1)

            def copies(g):
                ts = slice(g * GT, (g + 1) * GT)
                act.wait_ge(s_cf, g + 1)
                act.activation(ch[:, ts, :], cf[:, ts, :], ACT.Copy).then_inc(s_ch, 1)
                act.wait_ge(s_qn, g + 1)
                act.activation(qn[:, ts, QL:256], qn[:, ts, P:QL], ACT.Copy).then_inc(s_qd, 1)

            def high_kq(t):
                act.wait_ge(s_qk, t + 1)
                src = bank[4 + t % 2]
                for j, dst in enumerate((kTh, R1, R3)):
                    c = act.activation(dst[:, t * P:(t + 1) * P], src[:, j * P:(j + 1) * P], ACT.Copy)
                c.then_inc(s_qkh, 1)

            def high(it, item):
                kind, i = item
                r = RING[item]
                src = rBank[r % 2]
                if kind == "A":
                    act.wait_ge(s_full, W(it, r + 1, RPI))
                    act.activation(QWh[i % 2][:, :, :, 0:KL], src[:, 0:4 * KL].rearrange("p (c h k) -> p c h k", c=2, h=2),
                                   ACT.Copy).then_inc(s_hi, 1)
                if kind == "q":
                    act.wait_ge(s_full, W(it, r + 1, RPI))
                    if i >= 2:
                        act.wait_ge(s_ql, W(it, i - 1, UPI))
                    act.activation(q32[i % 2][:, :], src[:, :], ACT.Copy).then_inc(s_qc, 1)
                if kind == "M":
                    act.wait_ge(s_full, W(it, r + 1, RPI))
                    act.activation(Mh[:, i % GP, :], src[:, :], ACT.Identity, scale=kvs[:, 0:1]).then_inc(s_hi, 1)
                if kind == "OT":
                    act.wait_ge(s_full, W(it, r + 1, RPI))
                    act.activation(OTh[:, (i // B) % GP, (i % B) * S:(i % B + 1) * S], src[:, :], ACT.Copy).then_inc(s_hi, 1)

            def high_rope_weights(it, p):
                act.wait_ge(s_wa[p % 2], W(it, 16 * (p // 2 + 1), 16 * GP // 2))
                if p >= 2:
                    act.wait_ge(s_full, W(it, RING["q", 4 * p - 5] + 1, RPI))
                act.activation(QWh[p % 2][:, :, :, KL:P],
                               WA[p % 2][:, wR:wR + 4 * ROPE].rearrange("p (c h k) -> p c h k", c=2, h=2),
                               ACT.Copy).then_inc(s_wrh, 1)

            def high_query(it, u):
                act.wait_ge(s_qa, W(it, u + 1, UPI))
                if u >= 4:
                    act.wait_ge(s_S, W(it, NQ * (u - 3), SPI))
                act.activation(qh[u % 4][:, :], q32[u % 2][:, :], ACT.Copy).then_inc(s_qh, 1)

            def exps(it, n):
                u, qt = unit_of(n), n % NQ
                w = (qt + 1) * P
                act.wait_ge(s_max, W(it, n + 1, SPI))
                act.activation(Pr[n % 4][:, 0:w], sBank[n % 2][:, 0:w], ACT.Exp, bias=nmax[:, n % 8:n % 8 + 1],
                               scale=1.0, accum_out=sums[:, (u // 2) % 4, qt * HP + u % 2:qt * HP + u % 2 + 1])\
                   .then_inc(s_exp, 1)

            def high_probs(it, n):
                w = (n % NQ + 1) * P
                act.wait_ge(s_T, W(it, n + 1, SPI))
                if n >= 4:
                    act.wait_ge(s_PV, W(it, n - 3, SPI))
                act.activation(Ph[n % 4][:, 0:w], tBank[n % 2][:, 0:w], ACT.Copy, scale=PS).then_inc(s_ph, 1)

            def high_wb(i):
                act.activation(wbh[:, 2 * i:2 * i + 2, :], wbraw[:, 2 * i:2 * i + 2, :], ACT.Copy).then_inc(s_wbh, 1)

            act.wait_ge(s_eps, 1)
            act.activation(early_root[:, :], eps[:, :], ACT.Sqrt)
            root(0)
            root(1)
            high_w1(0)
            high_x(0)
            high_w1(1)
            for t in range(NT):
                if t + 2 < NT:
                    root(t + 2)
                if t + 1 < NT:
                    high_x(t + 1)
                if t in (2, 4, 6):
                    rms_roots(t // 2 - 1)
                if t in (4, 6):
                    high_kq(t - 4)
                    high_kq(t - 3)
                copy_projection(t)
                if t in (0, 1):
                    act.wait_ge(s_wbd, 16)
                    high_wb(t)
                if t in (2, 4, 6):
                    copies(t // 2 - 1)
                if t == 4:
                    high_rope_weights(0, 0)
                    high(0, ("A", 0))
            rms_roots(3)
            high_query(0, 0)
            copies(3)
            high_kq(4)
            high_kq(5)
            high_kq(6)
            high_kq(7)
            high_query(0, 1)
            act.wait_ge(s_ed, 1)
            act.activation(eg[:, :], gap[:, :], ACT.Exp).then_inc(s_ex, 1)

            def step(it, k, s):
                n = SPI * k + s
                high_probs(it, n)
                for kind, i in fillers(k, s):
                    if kind == "A":
                        high_rope_weights(it, i)
                for item in fillers(k, s - 1) if s else ():
                    if item[0] != "q":
                        high(it, item)
                if n + 2 < NN:
                    exps(it, n + 2)
                for item in fillers(k, s):
                    if item[0] == "q":
                        high(it, item)
                if s % 4 == 3 and UPI * k + s // 4 + 2 < NU:
                    high_query(it, UPI * k + s // 4 + 2)

            exps(0, 0)
            exps(0, 1)
            for s in range(SPI):
                step(0, 0, s)
            with act.Fori(1, NI - 1) as i:
                for s in range(SPI):
                    step(i, 1, s)
            def sigmoid(t):
                act.activation(sig[t], gate[:, t, :], ACT.Sigmoid).then_inc(s_sig, 1)

            for s in range(SPI):
                step(NI - 1, NI - 1, s)
                if s >= SPI - 2:
                    for t in range(NT)[2 * (s - SPI + 2):(2 if s < SPI - 1 else NT)]:
                        sigmoid(t)
            high(0, ("OT", NO - 1))

        @block.gpsimd
        def _(pool):
            chain = [0]

            def link(ins):
                chain[0] += 1
                ins.then_inc(s_pool, 1)
                pool.wait_ge(s_pool, chain[0])

            def rope_weights(it, p):
                pool.wait_ge(s_wrh, W(it, p + 1, GP))
                raw = WA[p % 2][:, wR:wR + 4 * ROPE].rearrange("p (c h k) -> p c h k", c=2, h=2)
                hi, lo = QWh[p % 2][:, :, :, KL:P], QWl[p % 2][:, :, :, KL:P]
                pool.tensor_tensor(lo, raw, hi.bitcast(f32), ALU.subtract).then_inc(s_wr, 1)

            def rope(it, u):
                i = u % 2
                pool.wait_ge(s_ql, W(it, u, UPI))
                if u % 4 == 3 and u // 4 + 1 < NP:
                    pool.wait_ge(s_wr, W(it, (u + 1) // 4 + 1, GP))
                pool.wait_ge(s_sw[i], W(it, 32 * ((u - 3) // 2 + 1), 32 * UPI // 2))
                pool.tensor_tensor(q32[i][KL:P, :], q32[i][KL:P, :], CQ[KL:P, :], ALU.mult)
                pool.tensor_tensor(qs[i][KL:P, :], qs[i][KL:P, :], SQ[KL:P, :], ALU.mult).then_inc(s_qv, 1)
                pool.wait_ge(s_qv, W(it, u + 1, UPI))
                pool.tensor_tensor(q32[i][KL:P, :], q32[i][KL:P, :], qs[i][KL:P, :], ALU.add).then_inc(s_qa, 1)
                low_query(it, u)

            def keys(g):
                ts, pos = slice(g * GT, (g + 1) * GT), slice(g * GT % NQ, g * GT % NQ + GT)
                pool.wait_ge(s_prc, (g + 1) * GT)
                xk = pr[:, ts, cK:cK + ROPE]
                xe = xk.rearrange("p t (j a) -> p t j a", a=2)
                se = SK[:, pos, :].rearrange("p t (j a) -> p t j a", a=2)
                te = t2[:, ts, :].rearrange("p t (j a) -> p t j a", a=2)
                pool.tensor_tensor(kc[:, ts, KL:], xk, CK[:, pos, :], ALU.mult)
                pool.tensor_tensor(te[:, :, :, 0], xe[:, :, :, 1], se[:, :, :, 0], ALU.mult)
                link(pool.tensor_tensor(te[:, :, :, 1], xe[:, :, :, 0], se[:, :, :, 1], ALU.mult))
                pool.tensor_tensor(kc[:, ts, KL:], kc[:, ts, KL:], t2[:, ts, :], ALU.add)
                pool.wait_ge(s_cf, g + 1)
                pool.tensor_tensor(kc[:, ts, 0:KL], cf[:, ts, :], kvw_s[:, :].unsqueeze(1).to_broadcast([P, GT, KL]),
                                   ALU.mult).then_inc(s_kc, 1)
                pool.wait_ge(s_ch, g + 1)
                link(pool.tensor_tensor(cl[:, ts, :], cf[:, ts, :], ch[:, ts, :], ALU.subtract))

            def low_query(it, u):
                pool.wait_ge(s_qh, W(it, u + 1, UPI))
                pool.tensor_tensor(ql[u % 4][:, :], q32[u % 2][:, :], qh[u % 4][:, :].bitcast(f32), ALU.subtract)\
                    .then_inc(s_ql, 1)

            def finish_rope(u):
                i = u % 2
                if u == 1:
                    pool.wait_ge(s_ql, 1)
                if u == 2:
                    pool.wait_ge(s_hw, 1)
                pool.wait_ge(s_qc, u + 1)
                pool.tensor_tensor(qs[i][KL:P, :], qs[i][KL:P, :], SQ[KL:P, :], ALU.mult).then_inc(s_qv, 1)
                pool.wait_ge(s_qv, u + 1)
                pool.tensor_tensor(q32[i][KL:P, :], q32[i][KL:P, :], qs[i][KL:P, :], ALU.add).then_inc(s_qa, 1)
                pool.wait_ge(s_qa, u + 1)

            pool.memset(eps[:, :], EPS_LN).then_inc(s_eps, 1)
            pool.wait_ge(s_kconst, 16 * 4)
            link(pool.tensor_scalar(kvw_s[:, :], kvwb[:, :], float(NOPE + ROPE) ** -0.5, 1.0, ALU.mult, ALU.mult))
            for t in range(NT - 1):
                if t in (0, 1, 3, 5):
                    k = (0, 1, 3, 5).index(t)
                    pool.wait_ge(s_wbh, k // 2 + 1)
                    pool.tensor_tensor(wbl[:, k, :], wbraw[:, k, :], wbh[:, k, :].bitcast(f32), ALU.subtract)\
                        .then_inc(s_wbl, 1)
                if t in (2, 4, 6):
                    keys(t // 2 - 1)
                if t == 4:
                    rope_weights(0, 0)
            finish_rope(0)
            keys(3)
            low_query(0, 0)
            finish_rope(1)
            low_query(0, 1)
            pool.wait_ge(s_wt, 1)
            pool.tensor_tensor(hw[:, :, :].rearrange("p t (e r) -> p (t e) r", e=NE),
                               pr[:, :, cH:cH + NE * R].rearrange("p t (e r) -> p t e r", e=NE),
                               oh[:, 0, :, :].unsqueeze(3).to_broadcast([P, NT, NE, R]), ALU.mult).then_inc(s_hw, 1)
            finish_rope(2)
            low_query(0, 2)

            def step(it, k, s):
                for kind, i in fillers(k, s):
                    if kind == "A":
                        rope_weights(it, i)
                for kind, i in fillers(k, s - 1) if s else ():
                    if kind == "q":
                        rope(it, i)

            for s in range(SPI):
                step(0, 0, s)
            with pool.Fori(1, NI - 1) as i:
                for s in range(SPI):
                    step(i, 1, s)
            for s in range(SPI):
                step(NI - 1, NI - 1, s)
            for t in range(NT - GV):
                pool.wait_ge(s_sig, t + 1)
                pool.tensor_tensor(gate[:, t, :], gate[:, t, :], sig[t], ALU.mult).then_inc(s_g, 1)
            pool.wait_ge(s_xr, 16)
            for t in range(NT - 1):
                pool.wait_ge(s_fm, t + 1)
                pool.tensor_tensor(acc[:, t, :], acc[:, t, :], xres[t], ALU.add).then_inc(s_fx, 1)

        @block.vector
        def _(dve):
            chain = [0]

            def link(ins):
                chain[0] += 1
                ins.then_inc(s_dv, 1)
                dve.wait_ge(s_dv, chain[0])

            def variance(t):
                dve.wait_ge(s_x[t], 16)
                link(dve.bn_stats(stats[:, t, :], xin[t % 4][:, :]))
                dve.bn_aggr(mv[:, t, :], stats[:, t, :]).then_inc(s_varq, 1)

            def normalise(t):
                dve.wait_ge(s_sq, t + 1)
                link(dve.reciprocal(rstd[:, t:t + 1], rstd[:, t:t + 1]))
                if t >= 2:
                    dve.wait_ge(s_xt, t - 1)
                dve.tensor_scalar(xn[t % 2][:, :], xin[t % 4][:, :], mv[:, t, 0:1], rstd[:, t:t + 1],
                                  ALU.subtract, ALU.mult).then_inc(s_xn, 1)

            def low_x(t):
                dve.wait_ge(s_xh, t + 1)
                tok = slice(t * P, (t + 1) * P)
                dve.tensor_tensor(xTl[:, :, tok], bank[t % 2][:, :].rearrange("p (k t) -> p k t", k=KD),
                                  xTh[:, :, tok].bitcast(f32), ALU.subtract).then_inc(s_xl, 1)

            def squares(t):
                dve.wait_ge(s_prc, t + 1)
                dve.tensor_tensor_reduce(qn[:, t, 0:QL], pr[:, t, cQ:cQ + QL], pr[:, t, cQ:cQ + QL], 1.0 / QL, EPS_RMS,
                                         ALU.mult, ALU.add, ms[:, t, 0:1])
                ins = dve.tensor_tensor_reduce(cf[:, t, :], pr[:, t, cC:cC + KL], pr[:, t, cC:cC + KL], 1.0 / KL, EPS_RMS,
                                               ALU.mult, ALU.add, ms[:, t, 1:2])
                if t % GT == GT - 1:
                    ins.then_inc(s_ms, 1)

            def latents(g):
                ts = slice(g * GT, (g + 1) * GT)
                dve.wait_ge(s_rms, g + 1)
                link(dve.reciprocal(ms[:, ts, :], ms[:, ts, :]))
                for t in range(g * GT, (g + 1) * GT):
                    ins = dve.tensor_scalar(cf[:, t, :], pr[:, t, cC:cC + KL], ms[:, t, 1:2], None, ALU.mult)
                ins.then_inc(s_cf, 1)
                for t in range(g * GT, (g + 1) * GT):
                    ins = dve.scalar_tensor_tensor(out=qn[:, t, 0:QL], in0=pr[:, t, cQ:cQ + QL], scalar=ms[:, t, 0:1],
                                                   in1=qwb[:, :], op0=ALU.mult, op1=ALU.mult)
                ins.then_inc(s_qn, 1)

            def low_w1(i):
                dve.wait_ge(s_w1h, i + 1)
                dve.tensor_tensor(w1l[:, 2 * i:2 * i + 2, :], w1raw[:, 2 * i:2 * i + 2, :],
                                  w1h[:, 2 * i:2 * i + 2, :].bitcast(f32), ALU.subtract).then_inc(s_w1l, 1)

            def low_kq(t):
                dve.wait_ge(s_qkh, t + 1)
                src = bank[4 + t % 2]
                c = slice(t * P, (t + 1) * P)
                dve.tensor_tensor(kTl[:, c], src[:, 0:P], kTh[:, c].bitcast(f32), ALU.subtract)
                dve.tensor_tensor(R2[:, c], src[:, P:2 * P], R1[:, c].bitcast(f32), ALU.subtract)
                dve.tensor_tensor(R3[KL:P, c], src[KL:P, 2 * P:3 * P], R3[KL:P, c].bitcast(f32), ALU.subtract)\
                   .then_inc(s_qkl, 1)

            def drain(it, item):
                kind, i = item
                r = RING[item]
                src = rBank[r % 2]
                if kind == "A":
                    dve.wait_ge(s_hi, W(it, HI[item] + 1, HPI))
                    dst = QWh[i % 2][:, :, :, 0:KL]
                    dve.tensor_tensor(QWl[i % 2][:, :, :, 0:KL], src[:, 0:4 * KL].rearrange("p (c h k) -> p c h k", c=2, h=2),
                                      dst.bitcast(f32), ALU.subtract).then_inc(s_drained, 1)
                if kind == "M":
                    dve.wait_ge(s_hi, W(it, HI[item] + 1, HPI))
                    dve.scalar_tensor_tensor(out=Ml[:, i % GP, :], in0=src[:, :], scalar=kvs[:, 0:1],
                                             in1=Mh[:, i % GP, :].bitcast(f32), op0=ALU.mult, op1=ALU.subtract)\
                       .then_inc(s_drained, 1)
                if kind == "OT":
                    dve.wait_ge(s_hi, W(it, HI[item] + 1, HPI))
                    j, c = (i // B) % GP, slice((i % B) * S, (i % B + 1) * S)
                    dve.tensor_tensor(OTl[:, j, c], src[:, :], OTh[:, j, c].bitcast(f32), ALU.subtract)\
                       .then_inc(s_drained, 1)
                if kind == "HT":
                    dve.wait_ge(s_full, r + 1)
                    dve.tensor_copy(hwT[:, 4 * i:4 * i + 4, :], src[:, :].rearrange("p (t c) -> p t c", t=4))\
                       .then_inc(s_drained, 1)
                if kind == "ffn":
                    dve.wait_ge(s_full, r + 1)
                    dve.tensor_tensor(gate[:, i, :], src[:, :], gate[:, i, :] if i < NB else bbb[:, :], ALU.add)\
                       .then_inc(s_drained, 1)
                if kind == "out":
                    t = i % NT
                    dve.wait_ge(s_full, W(it, r + 1, RPI))
                    if not isinstance(it, int):
                        dve.wait_ge(s_acc0, NT)
                    dve.tensor_tensor(acc[:, t, :], acc[:, t, :], src[:, :], ALU.add).then_inc(s_drained, 1)

            def first_rope(u):
                i, src = u % 2, rBank[RING["q", u] % 2]
                dve.wait_ge(s_full, RING["q", u] + 1)
                if u >= 2:
                    dve.wait_ge(s_ql, u - 1)
                dve.stream_shuffle(qs[i][KL:P, :], src[KL:P, :], SWAP)
                dve.tensor_tensor(q32[i][:, :], src[:, :], CQ[:, :], ALU.mult).then_inc(s_qc, 1)

            def drain_base(t):
                dve.wait_ge(s_base, t + 1)
                dve.tensor_tensor(gate[:, t, :], tBank[t % 2][:, :], bbb[:, :], ALU.add).then_inc(s_based, 1)

            variance(0)
            variance(1)
            normalise(0)
            normalise(1)
            low_w1(0)
            low_x(0)
            low_w1(1)
            variance(2)
            for t in range(NT):
                if t + 2 < NT:
                    normalise(t + 2)
                if t + 3 < NT:
                    variance(t + 3)
                if t + 1 < NT:
                    low_x(t + 1)
                if t == 0:
                    dve.wait_ge(s_kconst, 16 * 4)
                if t in (2, 4, 6):
                    latents(t // 2 - 1)
                if t in (4, 6):
                    low_kq(t - 4)
                    low_kq(t - 3)
                squares(t)
                dve.max(top[:, t, :], pr[:, t, cL:cL + NE])
                if t == 4:
                    drain(0, START[0])
                if t == 6:
                    dve.wait_ge(s_const, 16 * CONSTS)
                    first_rope(0)
            latents(3)
            low_kq(4)
            low_kq(5)
            dve.tensor_tensor(gap[:, :], top[:, :, 1], top[:, :, 0], ALU.subtract).then_inc(s_ed, 1)
            for t in range(NT):
                ins = dve.max_index(topi[:, t, :], top[:, t, :], pr[:, t, cL:cL + NE])
            link(ins)
            first_rope(1)
            drain_base(0)
            low_kq(6)
            low_kq(7)
            drain_base(1)
            dve.tensor_scalar(kvs[:, :], kvcol[:, :], 1.0 / PS, None, ALU.mult)
            link(dve.tensor_copy(idx[:, :, :], topi[:, :, 0:2]))
            row = iota[:, :].unsqueeze(1).to_broadcast([P, NT, NE])
            for j in range(2):
                dve.tensor_tensor(oh[:, j, :, :], row, idx[:, :, j:j + 1].to_broadcast([P, NT, NE]), ALU.is_equal)
            dve.wait_ge(s_ex, 1)
            link(dve.tensor_scalar(p12[:, 1, :], eg[:, :], 1.0, 1.0 / LORA_SCALE, ALU.add, ALU.mult))
            link(dve.reciprocal(p12[:, 0, :], p12[:, 1, :]))
            link(dve.tensor_tensor(p12[:, 1, :], eg[:, :], p12[:, 0, :], ALU.mult))
            for j in range(2):
                ins = dve.tensor_tensor(oh[:, j, :, :], oh[:, j, :, :],
                                        p12[:, j, :].unsqueeze(2).to_broadcast([P, NT, NE]), ALU.mult)
            link(ins)
            dve.tensor_tensor(oh[:, 0, :, :], oh[:, 0, :, :], oh[:, 1, :, :], ALU.add).then_inc(s_wt, 1)

            def row_max(it, n):
                w = (n % NQ + 1) * P
                dve.wait_ge(s_S, W(it, n + 1, SPI))
                dve.tensor_reduce(nmax[:, n % 8:n % 8 + 1], sBank[n % 2][:, 0:w], AX.X, ALU.max, negate=True)\
                   .then_inc(s_max, 1)

            def low_probs(it, n):
                w = (n % NQ + 1) * P
                dve.wait_ge(s_ph, W(it, n + 1, SPI))
                dve.scalar_tensor_tensor(out=Pl[n % 4][:, 0:w], in0=tBank[n % 2][:, 0:w], scalar=PS,
                                         in1=Ph[n % 4][:, 0:w], op0=ALU.mult, op1=ALU.subtract).then_inc(s_pl, 1)

            def normalise_block(it, ob):
                dve.wait_ge(s_PV, W(it, NQ * HP * (ob + 1), SPI))
                dve.reciprocal(rinv[:, ob % 2, :], sums[:, ob % 4, :]).then_inc(s_ri, 1)
                dve.wait_ge(s_ri, W(it, ob + 1, OPI))
                dve.tensor_tensor(osb[ob % 2][:, :, :].rearrange("p q (h c) -> p (q h) c", h=HP),
                                  oBank[ob % 2][:, :].rearrange("p (m c) -> p m c", c=KL),
                                  rinv[:, ob % 2, :].unsqueeze(2).to_broadcast([P, NQ * HP, KL]), ALU.mult)\
                   .then_inc(s_o, 1)

            def step(it, k, s):
                n = SPI * k + s
                if n + 2 < NN:
                    row_max(it, n + 2)
                for item in fillers(k, s - 1) if s else ():
                    drain(it, item)
                low_probs(it, n)
                if s % 8 == 3 and n > 8:
                    normalise_block(it, OPI * k + s // 8 - 1)

            row_max(0, 0)
            row_max(0, 1)
            drain_base(2)
            first_rope(2)
            drain_base(3)
            for s in range(SPI):
                step(0, 0, s)
                if s >= SPI - NT:
                    dve.memset(acc[:, s - SPI + NT, :], 0.0).then_inc(s_acc0, 1)
            with dve.Fori(1, NI - 1) as i:
                for s in range(SPI):
                    step(i, 1, s)
            for s in range(SPI):
                step(NI - 1, NI - 1, s)
            normalise_block(0, NO - 1)

            def apply_gate(t):
                dve.wait_ge(s_drained, DR["out", NT * (NI - 1) + t])
                if t < NT - GV:
                    dve.wait_ge(s_g, t + 1)
                dve.tensor_tensor(acc[:, t, :], acc[:, t, :], gate[:, t, :], ALU.mult).then_inc(s_fm, 1)

            for j, item in enumerate(DRAIN):
                drain(0, item)
                if j == 1:
                    for t in range(NT - GV, NT):
                        dve.wait_ge(s_sig, t + 1)
                        ins = dve.tensor_tensor(gate[:, t, :], gate[:, t, :], sig[t], ALU.mult)
                    link(ins)
                if j in (1, 2) or j > 3:
                    apply_gate(j - 1 if j < 3 else j - 2)
            apply_gate(NT - 1)
            dve.wait_ge(s_fm, NT)
            dve.wait_ge(s_xr, 16)
            dve.tensor_tensor(acc[:, NT - 1, :], acc[:, NT - 1, :], xres[NT - 1], ALU.add).then_inc(s_last, 1)


HI = {}
for _item in RING:
    if _item[0] in ("A", "M", "OT"):
        HI[_item] = len(HI)
HPI = 2 * GP + OPI

_OUTS = [((B, S, D), "float32")]


def _tables():
    import numpy as np
    freqs = (1.0 / 10000.0 ** (np.arange(0, ROPE, 2, dtype=np.float32) / np.float32(ROPE))).astype(np.float32)
    ang = np.outer(np.arange(S, dtype=np.float32), freqs).astype(np.float32)
    cos, sin = np.cos(ang).astype(np.float32), np.sin(ang).astype(np.float32)
    c2 = np.repeat(cos, 2, axis=1)
    s2 = np.stack([-sin, sin], axis=-1).reshape(S, ROPE)
    scale = np.float32(float(NOPE + ROPE) ** -0.5)
    cosq = np.concatenate([np.ones((KL, S), np.float32), c2.T], axis=0)
    sinq = np.concatenate([np.zeros((KL, S), np.float32), s2.T], axis=0)
    cosk = (c2 * scale).reshape(NQ, P, ROPE).transpose(1, 0, 2)
    sink = (s2 * scale).reshape(NQ, P, ROPE).transpose(1, 0, 2)
    mask = np.triu(np.full((P, P), MASKED, np.float32), 1)
    return cosq, sinq, cosk, sink, np.eye(P, dtype=np.float32), mask, np.tile(np.arange(NE, dtype=np.float32), (P, 1))


def kernel(**inputs):
    import numpy as np
    import ml_dtypes
    import concourse.bacc as _bacc
    from concourse.bass_utils import run_bass_kernel_spmd as _run

    a = {k.replace("L0_attn_", "").replace("L0_ffn_", ""): np.asarray(v) for k, v in inputs.items()}

    def by_rows(w):
        return w.reshape(KD, P, -1).transpose(1, 0, 2)

    w1 = by_rows(np.concatenate([a["wq_a"].T, a["wkv_a"].T, a["lora_A"].reshape(NE * R, D).T, a["W_router"].T], axis=1))
    wb = by_rows(a["W_base"].T)
    lbt = a["lora_B"].transpose(0, 2, 1).reshape(NE * R, D)
    wqb = a["wq_b"].reshape(NP, HP, NOPE + ROPE, QL)
    nope = wqb[:, :, :NOPE, :].transpose(0, 2, 1, 3)
    nope = np.concatenate([nope, nope[..., P:QL]], axis=-1).reshape(NP, P, HP * 256)
    rope = wqb[:, :, NOPE:, :].transpose(0, 3, 1, 2)
    rope = np.stack([rope[:, 0:P], np.concatenate([rope[:, P:QL], rope[:, P:QL]], axis=1)], axis=2)
    rope = rope.reshape(NP, P, 2 * HP * ROPE)
    wkv = a["wkv_b"].reshape(NP, HP, 2, P, KL).transpose(0, 3, 2, 1, 4).reshape(NP, P, 2 * HP * KL)
    wo = a["wo"].T.reshape(NP, HP, VD, D).transpose(0, 2, 1, 3).reshape(NP, P, HP * D)
    wp = np.concatenate([nope, rope, wkv, wo], axis=-1)
    cosq, sinq, cosk, sink, ident, mask, iota = _tables()
    arrays_in = [a["x"], w1, wb, lbt, wp, a["q_norm_w"], a["kv_norm_w"], a["b_base"], cosq, sinq, cosk, sink,
                 ident, mask.astype(ml_dtypes.bfloat16), ident.astype(ml_dtypes.bfloat16), iota]
    names = ["x", "w1", "wb", "lbt", "wp", "qw", "kvw", "bb", "cosq", "sinq", "cosk", "sink", "ident", "mask",
             "identb", "iota"]
    nc = _bacc.Bacc("TRN2", target_bir_lowering=False, num_devices=1)
    arrays, args = {}, []
    for name, v in zip(names, arrays_in):
        v = np.ascontiguousarray(v)
        arrays[f"in_{name}"] = v
        args.append(nc.dram_tensor(f"in_{name}", v.shape, mybir.dt.from_np(v.dtype), kind="ExternalInput").ap())
    args.append(nc.dram_tensor("out_0", _OUTS[0][0], f32, kind="ExternalOutput").ap())
    attention_kernel(nc, *args)
    r = _run(nc, [arrays], core_ids=[0])
    return r.results[0]["out_0"]
```
